# Optimizing a Trainium2 kernel written in Bass

```python
import numpy as np
import jax
import jax.numpy as jnp

def _softmax(x, axis=-1):
    return jax.nn.softmax(x, axis=axis)

def _gelu(x):
    return jax.nn.gelu(x, approximate=True)

def _silu(x):
    return jax.nn.silu(x)

def _sigmoid(x):
    return jax.nn.sigmoid(x)

def _layernorm(x, axis=-1, eps=1e-05):
    m = jnp.mean(x, axis=axis, keepdims=True)
    v = jnp.var(x, axis=axis, keepdims=True)
    return (x - m) / jnp.sqrt(v + eps)

def _scatter_add(tgt, idx, src, axis=0):
    return tgt.at[idx].add(src)

def _segment_sum(src, seg, n):
    return jax.ops.segment_sum(src, seg, n)
kernel_name = 'mk_gnn_preln_d1_gnn_r32_5a95ae'

def setup_inputs(seed: int=0):
    np.random.seed(seed)
    _w = jnp.asarray

    def _rec_inputs():
        import jax
        import jax.numpy as jnp
        _gk = jax.random.key(seed)
        x = -0.000202 + 1 * jax.random.normal(jax.random.fold_in(_gk, 1), (50000, 128), jnp.float32)
        src = jax.random.randint(jax.random.fold_in(_gk, 2), (50000,), 0, 50000, jnp.int32)
        dst = jax.random.randint(jax.random.fold_in(_gk, 3), (50000,), 0, 50000, jnp.int32)
        _o = jnp.argsort(dst, stable=True)
        src = src[_o]
        dst = dst[_o]
        return (x, src, dst)
    x, src, dst = _rec_inputs()

    def _L0_gnn_setup():
        import jax, jax.numpy as jnp
        import numpy as np
        N_NODES = 50000
        N_EDGES = 25000
        LATDIM = 128
        HEAD = 4
        key = jax.random.key(seed)
        k1, k2, k3, k4, k5, k6 = jax.random.split(key, 6)
        scale = 1.0 / np.sqrt(LATDIM)
        return {'embeds': jax.random.normal(k1, (N_NODES, LATDIM), dtype=jnp.float32), 'qW': jax.random.normal(k2, (LATDIM, LATDIM), dtype=jnp.float32) * scale, 'kW': jax.random.normal(k3, (LATDIM, LATDIM), dtype=jnp.float32) * scale, 'vW': jax.random.normal(k4, (LATDIM, LATDIM), dtype=jnp.float32) * scale, 'rows': jax.random.randint(k5, (N_EDGES,), 0, N_NODES, dtype=jnp.int32), 'cols': jax.random.randint(k6, (N_EDGES,), 0, N_NODES, dtype=jnp.int32)}
    _L0_gnn_all = _L0_gnn_setup()
    _L0_gnn_in = {k: v for k, v in _L0_gnn_all.items() if k in ('qW', 'kW', 'vW')}
    del _L0_gnn_all
    return {'x': x, 'src': src, 'dst': dst, 'L0_gnn_qW': _L0_gnn_in['qW'], 'L0_gnn_kW': _L0_gnn_in['kW'], 'L0_gnn_vW': _L0_gnn_in['vW']}

def reference(x, src, dst, L0_gnn_qW, L0_gnn_kW, L0_gnn_vW):
    import jax
    import jax.numpy as jnp

    def _L0_gnn_ref(embeds, qW, kW, vW, rows, cols):
        import jax, jax.numpy as jnp
        import numpy as np
        N_NODES = 50000
        N_EDGES = 25000
        LATDIM = 128
        HEAD = 4
        n_nodes, latdim = embeds.shape
        head_dim = latdim // HEAD
        rowEmb = embeds[rows]
        colEmb = embeds[cols]
        q = (rowEmb @ qW).reshape(-1, HEAD, head_dim)
        k = (colEmb @ kW).reshape(-1, HEAD, head_dim)
        v = (colEmb @ vW).reshape(-1, HEAD, head_dim)
        att = jnp.einsum('ehd,ehd->eh', q, k)
        att = jnp.clip(att, -10.0, 10.0)
        expAtt = jnp.exp(att)
        attNorm = jax.ops.segment_sum(expAtt, rows, num_segments=n_nodes)[rows]
        att = expAtt / (attNorm + 1e-08)
        res = (att[:, :, None] * v).reshape(-1, latdim)
        out = jax.ops.segment_sum(res, rows, num_segments=n_nodes)
        return out
    h = jnp.maximum(_layernorm(x, axis=-1), 0.0)
    x = x + _L0_gnn_ref(h, L0_gnn_qW, L0_gnn_kW, L0_gnn_vW, src, dst)
    return x

_drawn_inputs = setup_inputs


def setup_inputs(seed=0):
    import zlib

    import numpy as np

    out = dict(_drawn_inputs(seed))
    spreads = {}
    factors = {}
    for name, (base, spread) in spreads.items():
        noise = np.random.default_rng([zlib.crc32(name.encode()), seed]).standard_normal(out[name].shape)
        drawn = base * np.exp(spread * noise) if base else spread * noise
        out[name] = jnp.asarray(drawn.astype(out[name].dtype))
    for name, factor in factors.items():
        out[name] = (out[name] * factor).astype(out[name].dtype)
    return out
```

```python
from contextlib import ExitStack

import concourse.bass as bass
from concourse import mybir

F32 = mybir.dt.float32
I32 = mybir.dt.int32
ALU = mybir.AluOpType
ACT = mybir.ActivationFunctionType
AX_X = mybir.AxisListType.X

LN_EPS = 1e-5
NORM_EPS = 1e-8
CLIP = 10.0
LANES = 125
HEADS = 4


def gnn_kernel(nc, x, src, dst, qW, kW, vW, out):
    N, D = x.shape
    E = src.shape[0]
    T = E // LANES
    HD = D // HEADS
    W = D + HEADS
    ROWS = N // LANES
    RB = 4
    FAR = 65536

    acc = nc.dram_tensor("acc", [N, W], F32, kind="Internal").ap()
    src_lanes = src.rearrange("(p t) -> p t", p=LANES)
    dst_lanes = dst.rearrange("(p t) -> p t", p=LANES)
    acc_lanes = acc.rearrange("(p t) w -> p (t w)", p=LANES)
    x_lanes = x.rearrange("(p t) d -> p (t d)", p=LANES)
    out_lanes = out.rearrange("(p t) d -> p (t d)", p=LANES)

    with ExitStack() as ctx:
        def sb(name, shape, dt=F32):
            return ctx.enter_context(nc.sbuf_tensor(name, shape, dt))

        def psum(name, shape):
            return ctx.enter_context(nc.psum_tensor(name, shape, F32))

        def sem(name):
            return ctx.enter_context(nc.semaphore(name))

        ident = sb("ident", [128, 128])
        before = sb("before", [128, 128])
        q_w = sb("q_w", [128, D])
        kv_w = sb("kv_w", [128, 2 * D])
        eps_col = sb("eps_col", [128, 1])
        src_i = sb("src_i", [LANES, T], I32)
        dst_i = sb("dst_i", [LANES, T], I32)
        src_f = sb("src_f", [LANES, T])

        g_zero = sb("g_zero", [LANES, 20 * W])
        g_idx = sb("g_idx", [LANES, 2], I32)
        g_x = sb("g_x", [LANES, 2, D])
        g_acc = sb("g_acc", [LANES, W])
        g_stats = sb("g_stats", [LANES, 2, 6])
        g_mv = sb("g_mv", [LANES, 2, 2])
        g_rstd = sb("g_rstd", [LANES, 2, 2])
        g_hT = sb("g_hT", [128, 2, LANES])
        g_att = sb("g_att", [LANES, 2, HEADS])
        g_prod = sb("g_prod", [LANES, D])
        g_q = sb("g_q", [LANES, D])
        g_res = sb("g_res", [LANES, W])
        g_sb = sb("g_sb", [LANES, LANES])
        g_sel = sb("g_sel", [LANES, LANES])
        g_cnt = sb("g_cnt", [LANES, 1])
        g_to = sb("g_to", [LANES, 1], I32)
        g_new = sb("g_new", [LANES, W])
        f_acc = sb("f_acc", [LANES, RB, W])
        f_x = sb("f_x", [LANES, RB, D])
        f_r = sb("f_r", [LANES, RB, HEADS])
        f_o = sb("f_o", [LANES, RB, D])

        p_T = psum("p_T", [128, 512])
        p_S = psum("p_S", [128, 512])
        p_qkv = psum("p_qkv", [128, 512])
        p_agg = psum("p_agg", [128, 512])

        s_in = sem("s_in")
        s_passed = sem("s_passed")
        s_const = sem("s_const")
        s_masks = sem("s_masks")
        s_srcf = sem("s_srcf")
        sg_zero = sem("sg_zero")
        sg_cleared = sem("sg_cleared")
        sg_idx = sem("sg_idx")
        sg_gathered = sem("sg_gathered")
        sg_scattered = sem("sg_scattered")
        sg_stats = sem("sg_stats")
        sg_mv = sem("sg_mv")
        sg_ln = sem("sg_ln")
        sg_rstd = sem("sg_rstd")
        sg_norm = sem("sg_norm")
        sg_xT = sem("sg_xT")
        sg_hT = sem("sg_hT")
        sg_qkv = sem("sg_qkv")
        sg_q = sem("sg_q")
        sg_sb = sem("sg_sb")
        sg_sT = sem("sg_sT")
        sg_sel = sem("sg_sel")
        sg_cnt = sem("sg_cnt")
        sg_far = sem("sg_far")
        sg_to = sem("sg_to")
        sg_prod = sem("sg_prod")
        sg_att = sem("sg_att")
        sg_clip = sem("sg_clip")
        sg_exp = sem("sg_exp")
        sg_res = sem("sg_res")
        sg_agg = sem("sg_agg")
        sg_new = sem("sg_new")
        sf_done = sem("sf_done")
        sf_in = sem("sf_in")
        sf_r = sem("sf_r")
        sf_o = sem("sf_o")
        sf_out = sem("sf_out")

        block = ctx.enter_context(nc.Block())

        def hold(eng, semaphore, value):
            eng.wait_ge(semaphore, value)
            eng.sem_inc(s_passed, 1)

        def general_sync(sp):
            sp.wait_ge(sg_zero, 1)
            with sp.Fori(0, T // 20) as i:
                sp.dma_start(acc_lanes[:, bass.ds(i * (20 * W), 20 * W)], g_zero[:]).then_inc(sg_cleared, 16)
            sp.wait_ge(sf_done, 1)
            with sp.Fori(0, ROWS // RB) as i:
                sp.dma_start(f_acc[:].rearrange("p t w -> p (t w)"),
                             acc_lanes[:, bass.ds(i * (RB * W), RB * W)]).then_inc(sf_in, 16)
                sp.dma_start(f_x[:].rearrange("p t d -> p (t d)"),
                             x_lanes[:, bass.ds(i * (RB * D), RB * D)]).then_inc(sf_in, 16)
                sp.wait_ge(sf_o, 2 * i + 2)
                sp.dma_start(out_lanes[:, bass.ds(i * (RB * D), RB * D)],
                             f_o[:].rearrange("p t d -> p (t d)")).then_inc(sf_out, 16)
                hold(sp, sf_out, 16 * i + 16)

        def general_pool(pool):
            pool.wait_ge(sg_cleared, 16 * (T // 20))
            with pool.Fori(0, T) as i:
                pool.tensor_copy(g_idx[:, 0:1], src_i[:, bass.ds(i, 1)]).then_inc(sg_idx, 1)
                pool.tensor_copy(g_idx[:, 1:2], dst_i[:, bass.ds(i, 1)]).then_inc(sg_idx, 1)
                hold(pool, sg_idx, 2 * i + 2)
                at_src = bass.IndirectOffsetOnAxis(ap=g_idx[:, 0:1], axis=0)
                at_dst = bass.IndirectOffsetOnAxis(ap=g_idx[:, 1:2], axis=0)
                pool.indirect_dma_start(g_x[:, 0, :], None, x, at_src).then_inc(sg_gathered, 16)
                pool.indirect_dma_start(g_x[:, 1, :], None, x, at_dst).then_inc(sg_gathered, 16)
                pool.indirect_dma_start(g_acc[:], None, acc, at_src).then_inc(sg_gathered, 16)
                pool.wait_ge(sg_to, i + 1)
                hold(pool, sg_new, i + 1)
                pool.indirect_dma_start(acc, bass.IndirectOffsetOnAxis(ap=g_to[:, 0:1], axis=0), g_new[:], None,
                                        bounds_check=N - 1, oob_is_err=False).then_inc(sg_scattered, 16)
                hold(pool, sg_scattered, 16 * i + 16)
            pool.nop().then_inc(sf_done, 1)

        def general_vector(dve):
            dve.memset(g_zero[:], 0.0).then_inc(sg_zero, 1)
            with dve.Fori(0, T) as i:
                dve.tensor_copy(g_sb[:], src_f[:, bass.ds(i, 1)].to_broadcast([LANES, LANES])).then_inc(sg_sb, 1)
                dve.wait_ge(sg_gathered, 48 * i + 48)
                for k in range(2):
                    dve.bn_stats(g_stats[:, k, :], g_x[:, k, :]).then_inc(sg_stats, 1)
                hold(dve, sg_stats, 2 * i + 2)
                for k in range(2):
                    dve.bn_aggr(g_mv[:, k, :], g_stats[:, k, :]).then_inc(sg_mv, 1)
                dve.wait_ge(sg_sT, i + 1)
                dve.tensor_scalar(g_sel[:], p_S[0:LANES, 0:LANES], g_sb[:, 0:1], None,
                                  ALU.is_equal).then_inc(sg_sel, 1)
                dve.wait_ge(sg_sel, i + 1)
                dve.tensor_tensor_reduce(g_prod[:, 0:LANES], g_sel[:], before[0:LANES, 0:LANES], 1.0, 0.0, ALU.mult,
                                         ALU.add, g_cnt[:]).then_inc(sg_cnt, 1)
                dve.wait_ge(sg_cnt, i + 1)
                dve.scalar_tensor_tensor(g_to[:], g_cnt[:], float(FAR), g_sb[:, 0:1], ALU.mult,
                                         ALU.add).then_inc(sg_to, 1)
                dve.wait_ge(sg_rstd, i + 1)
                for k in range(2):
                    dve.tensor_scalar(g_x[:, k, :], g_x[:, k, :], g_mv[:, k, 0:1], g_rstd[:, 1, k:k + 1],
                                      ALU.subtract, ALU.mult).then_inc(sg_norm, 1)
                dve.wait_ge(sg_q, i + 1)
                dve.tensor_tensor(g_prod[:], g_q[:], p_qkv[0:LANES, D:2 * D],
                                  ALU.mult).then_inc(sg_prod, 1)
                dve.wait_ge(sg_prod, i + 1)
                dve.tensor_reduce(g_att[:, 0, :], g_prod[:].rearrange("p (h d) -> p h d", h=HEADS), AX_X,
                                  ALU.add).then_inc(sg_att, 1)
                dve.wait_ge(sg_att, i + 1)
                dve.tensor_scalar(g_att[:, 1, :], g_att[:, 0, :], -CLIP, CLIP, ALU.max, ALU.min).then_inc(sg_clip, 1)
                dve.wait_ge(sg_exp, i + 1)
                dve.tensor_tensor(g_res[:, 0:D].rearrange("p (h d) -> p h d", h=HEADS),
                                  p_qkv[0:LANES, 2 * D:3 * D].rearrange("p (h d) -> p h d", h=HEADS),
                                  g_res[:, D:W].unsqueeze(2).to_broadcast([LANES, HEADS, HD]),
                                  ALU.mult).then_inc(sg_res, 1)
                dve.wait_ge(sg_agg, i + 1)
                dve.tensor_tensor(g_new[:], p_agg[0:LANES, 0:W], g_acc[:], ALU.add).then_inc(sg_new, 1)
            with dve.Fori(0, ROWS // RB) as i:
                dve.wait_ge(sf_in, 32 * i + 32)
                dve.tensor_scalar(f_r[:], f_acc[:, :, D:W], NORM_EPS, None, ALU.add).then_inc(sf_r, 1)
                dve.wait_ge(sf_r, 2 * i + 1)
                dve.reciprocal(f_r[:], f_r[:]).then_inc(sf_r, 1)
                dve.wait_ge(sf_r, 2 * i + 2)
                for t in range(RB):
                    last = dve.tensor_tensor(f_o[:, t, :].rearrange("p (h d) -> p h d", h=HEADS),
                                             f_acc[:, t, 0:D].rearrange("p (h d) -> p h d", h=HEADS),
                                             f_r[:, t, :].unsqueeze(2).to_broadcast([LANES, HEADS, HD]), ALU.mult)
                last.then_inc(sf_o, 1)
                dve.wait_ge(sf_o, 2 * i + 1)
                dve.tensor_tensor(f_o[:], f_o[:], f_x[:], ALU.add).then_inc(sf_o, 1)

        def general_scalar(act):
            with act.Fori(0, T) as i:
                act.wait_ge(sg_mv, 2 * i + 2)
                act.activation(g_rstd[:, 0, :], g_mv[:, :, 1], ACT.Ln, bias=eps_col[0:LANES, :]).then_inc(sg_ln, 1)
                act.wait_ge(sg_ln, i + 1)
                act.activation(g_rstd[:, 1, :], g_rstd[:, 0, :], ACT.Exp, scale=-0.5).then_inc(sg_rstd, 1)
                act.wait_ge(sg_xT, i + 1)
                act.activation(g_hT[:], p_T[:, 0:2 * LANES].rearrange("p (k l) -> p k l", k=2),
                               ACT.Relu).then_inc(sg_hT, 1)
                act.wait_ge(sg_qkv, i + 1)
                act.activation(g_q[:], p_qkv[0:LANES, 0:D], ACT.Copy).then_inc(sg_q, 1)
                act.wait_ge(sg_clip, i + 1)
                act.activation(g_res[:, D:W], g_att[:, 1, :], ACT.Exp).then_inc(sg_exp, 1)

        def general_tensor(pe):
            with pe.Fori(0, T) as i:
                pe.wait_ge(sg_sb, i + 1)
                pe.transpose(p_S[0:LANES, 0:LANES], g_sb[:], ident[0:LANES, 0:LANES]).then_inc(sg_sT, 1)
                pe.wait_ge(sg_norm, 2 * i + 2)
                for k in range(2):
                    last = pe.transpose(p_T[:, k * LANES:(k + 1) * LANES], g_x[:, k, :], ident[0:LANES, 0:LANES])
                last.then_inc(sg_xT, 1)
                pe.wait_ge(sg_hT, i + 1)
                pe.matmul(p_qkv[0:LANES, 0:D], g_hT[:, 0, :], q_w[:], start=True, stop=True)
                pe.matmul(p_qkv[0:LANES, D:3 * D], g_hT[:, 1, :], kv_w[:], start=True, stop=True).then_inc(sg_qkv, 1)
                pe.wait_ge(sg_res, i + 1)
                pe.wait_ge(sg_sel, i + 1)
                pe.matmul(p_agg[0:LANES, 0:W], g_sel[:], g_res[:], start=True, stop=True).then_inc(sg_agg, 1)

        @block.sync
        def _(sp):
            sp.dma_start(src_i[:], src_lanes).then_inc(s_in, 16)
            sp.dma_start(dst_i[:], dst_lanes).then_inc(s_in, 16)
            sp.dma_start(q_w[:], qW).then_inc(s_in, 16)
            sp.dma_start(kv_w[:, 0:D], kW).then_inc(s_in, 16)
            sp.dma_start(kv_w[:, D:2 * D], vW).then_inc(s_in, 16)
            general_sync(sp)

        @block.gpsimd
        def _(pool):
            pool.memset(ident[:], 1.0).then_inc(s_const, 1)
            pool.memset(before[:], 1.0).then_inc(s_const, 1)
            pool.memset(eps_col[:], LN_EPS).then_inc(s_const, 1)
            pool.wait_ge(s_const, 3)
            pool.affine_select(out=ident[:], in_=ident[:], compare_op=ALU.is_equal, fill=0.0, base=0,
                               pattern=[[-1, 128]], channel_multiplier=1).then_inc(s_masks, 1)
            pool.affine_select(out=before[:], in_=before[:], compare_op=ALU.is_gt, fill=0.0, base=0,
                               pattern=[[-1, 128]], channel_multiplier=1).then_inc(s_masks, 1)
            pool.wait_ge(s_in, 80)
            general_pool(pool)

        @block.vector
        def _(dve):
            dve.wait_ge(s_in, 80)
            dve.wait_ge(s_masks, 2)
            dve.tensor_copy(src_f[:], src_i[:]).then_inc(s_srcf, 1)
            dve.wait_ge(s_srcf, 1)
            general_vector(dve)

        @block.scalar
        def _(act):
            act.preload_act_table_set("natural_log_exp_and_others")
            act.wait_ge(s_const, 3)
            general_scalar(act)

        @block.tensor
        def _(pe):
            pe.wait_ge(s_in, 80)
            pe.wait_ge(s_masks, 2)
            general_tensor(pe)


def kernel(x, src, dst, L0_gnn_qW, L0_gnn_kW, L0_gnn_vW):
    import numpy as np
    import concourse.bacc as bacc
    from concourse.bass_utils import run_bass_kernel_spmd

    nc = bacc.Bacc("TRN2", target_bir_lowering=False, num_devices=1)
    given = {"x": x, "src": src, "dst": dst, "qW": L0_gnn_qW, "kW": L0_gnn_kW, "vW": L0_gnn_vW}
    arrays, aps = {}, {}
    for name, a in given.items():
        a = np.ascontiguousarray(a)
        arrays[f"in_{name}"] = a
        aps[name] = nc.dram_tensor(f"in_{name}", a.shape, mybir.dt.from_np(a.dtype), kind="ExternalInput").ap()
    out = nc.dram_tensor("out", list(x.shape), F32, kind="ExternalOutput").ap()
    gnn_kernel(nc, aps["x"], aps["src"], aps["dst"], aps["qW"], aps["kW"], aps["vW"], out)
    r = run_bass_kernel_spmd(nc, [arrays], core_ids=[0])
    return r.results[0]["out"]
```

```python
from contextlib import ExitStack

import concourse.bass as bass
from concourse import mybir

F32 = mybir.dt.float32
BF16 = mybir.dt.bfloat16
I32 = mybir.dt.int32
ALU = mybir.AluOpType
ACT = mybir.ActivationFunctionType
AX_X = mybir.AxisListType.X

LN_EPS = 1e-5
NORM_EPS = 1e-8
CLIP = 10.0
HEADS = 4
LANES = 125
EG = 8
BUCKET = 98
SLOTS = 128


def gnn_kernel(nc, x, src, dst, qW, kW, vW, out):
    N, D = x.shape
    E = src.shape[0]
    T = E // LANES
    HD = D // HEADS
    W = D + HEADS
    ROWS = N // LANES
    RB = 4
    FAR = 65536

    NB = 512
    NP = NB // 2
    DEEP = 8
    NHOT = 4
    FIELDS = 3
    COLS = -(-NB // FIELDS)
    GB = 3
    FAR_SLOT = float(1 << 20)
    NG = T // EG
    GN = 128 * EG
    ND = N // GN
    LAST = (N - ND * GN) // EG
    TAIL = N - (NP - 1) * 2 * BUCKET
    assert N <= NB * BUCKET and 0 < TAIL <= BUCKET and T % EG == 0 and (N - ND * GN) % EG == 0
    assert 2 * SLOTS <= 256 and FIELDS * 8 <= 24 and ND == NG - 2 and ND % GB == 0 and NP % DEEP == 0

    h_dram = nc.dram_tensor("h_rows", [N, D], F32, kind="Internal").ap()
    q_dram = nc.dram_tensor("q_rows", [NB * BUCKET, D], F32, kind="Internal").ap()
    slots = nc.dram_tensor("slots", [2 * NB * SLOTS, 1], I32, kind="Internal").ap()
    slot_rows = slots.rearrange("(c b s) o -> b c (s o)", b=128, s=SLOTS)
    acc = nc.dram_tensor("acc", [N, W], F32, kind="Internal").ap()
    src_lanes = src.rearrange("(p t) -> p t", p=LANES)
    dst_lanes = dst.rearrange("(p t) -> p t", p=LANES)
    acc_lanes = acc.rearrange("(p t) w -> p (t w)", p=LANES)
    x_lanes = x.rearrange("(p t) d -> p (t d)", p=LANES)
    out_lanes = out.rearrange("(p t) d -> p (t d)", p=LANES)

    with ExitStack() as ctx:
        def sb(name, shape, dt=F32):
            return ctx.enter_context(nc.sbuf_tensor(name, shape, dt))

        def psum(name, shape):
            return ctx.enter_context(nc.psum_tensor(name, shape, F32))

        def sem(name):
            return ctx.enter_context(nc.semaphore(name))

        ident = sb("ident", [128, 128])
        before = sb("before", [128, 128])
        q_w = sb("q_w", [128, D])
        kv_w = sb("kv_w", [128, 2 * D])
        eps_col = sb("eps_col", [128, 1])
        src_i = sb("src_i", [LANES, T], I32)
        dst_i = sb("dst_i", [LANES, T], I32)
        src_f = sb("src_f", [LANES, T])

        bucket_f = sb("bucket_f", [LANES, T])
        place_f = sb("place_f", [LANES, T])
        fix_f = sb("fix_f", [LANES, T])
        bucket_i = sb("bucket_i", [LANES, T], I32)
        first_f = sb("first_f", [LANES, T])
        pay_f = sb("pay_f", [LANES, T])
        iota_i = sb("iota_i", [128, NB], I32)
        iota_b = sb("iota_b", [LANES, COLS], BF16)
        iota_f = sb("iota_f", [128, BUCKET])
        upto = sb("upto", [LANES, 2, LANES], BF16)
        col_f = sb("col_f", [LANES, T])
        unit_f = sb("unit_f", [LANES, T])
        inv_f = sb("inv_f", [LANES, T])
        shift_i = sb("shift_i", [LANES, T], I32)
        over_f = sb("over_f", [LANES, T])
        sign = sb("sign", [LANES, EG])
        e_hot = sb("e_hot", [LANES, NHOT, COLS], BF16)
        e_skip = sb("e_skip", [LANES, COLS])
        e_raw = sb("e_raw", [LANES, GB, EG])
        e_count = sb("e_count", [LANES, GB, EG], I32)
        e_field = sb("e_field", [LANES, GB, EG], I32)
        e_rank = sb("e_rank", [LANES, GB, EG], I32)
        e_in = sb("e_in", [LANES, GB, EG])
        e_off = sb("e_off", [LANES, GB, EG])
        e_slot = sb("e_slot", [LANES, GB, EG], I32)
        e_pay = sb("e_pay", [LANES, GB, EG], I32)
        zero_i = sb("zero_i", [128, 2 * NB], I32)
        zero_q = sb("zero_q", [128, 2 * D])
        zero_h = sb("zero_h", [LANES, COLS], BF16)
        upto_f = sb("upto_f", [LANES, 2, LANES])
        count_i = sb("count_i", [1, 2, COLS], I32)
        field_i = sb("field_i", [1, 2, FIELDS, COLS], I32)
        count_f = sb("count_f", [1, FIELDS * COLS])
        most_f = sb("most_f", [1, 1])
        full_f = sb("full_f", [1, 1])
        left_f = sb("left_f", [1, 1])
        one_col = sb("one_col", [128, 1])
        ones_f = sb("ones_f", [LANES, 1])
        osum_f = sb("osum_f", [LANES, 1])
        over_i = sb("over_i", [1, 1], I32)
        n_x = sb("n_x", [128, GB, EG, D])
        n_stats = sb("n_stats", [128, GB, EG, 6])
        n_mv = sb("n_mv", [128, GB, EG, 2])
        n_ln = sb("n_ln", [128, GB, EG])
        n_rstd = sb("n_rstd", [128, GB, EG])
        n_bias = sb("n_bias", [128, GB, EG])
        n_h = sb("n_h", [128, GB, EG, D])
        n_hT = sb("n_hT", [128, 2, 4 * 128])
        n_q = sb("n_q", [128, GB, EG, D])
        slot_i = sb("slot_i", [128, 2 * NB // 128, SLOTS], I32)
        slot_f = sb("slot_f", [128, NB // 128, SLOTS])
        pay_i = sb("pay_i", [SLOTS, NB], I32)
        dst_col = sb("dst_col", [SLOTS, NB], I32)
        place_i = sb("place_i", [SLOTS, NB], I32)
        place_col = sb("place_col", [SLOTS, NB])
        a_idx = sb("a_idx", [SLOTS, DEEP, 2], I32)
        a_h = sb("a_h", [SLOTS, DEEP, 2, D])
        a_q = sb("a_q", [BUCKET, DEEP, 2, D])
        a_x = sb("a_x", [BUCKET, DEEP, 2, D])
        a_hot = sb("a_hot", [SLOTS, DEEP, 2, BUCKET])
        a_off = sb("a_off", [SLOTS, 2, 2, BUCKET])
        a_T = sb("a_T", [128, 2, 4, 128])
        a_qe = sb("a_qe", [SLOTS, 2, 2, D])
        a_prod = sb("a_prod", [SLOTS, 2, 2, D])
        a_att = sb("a_att", [SLOTS, 2, 2, HEADS])
        a_clip = sb("a_clip", [SLOTS, 2, 2, HEADS])
        a_res = sb("a_res", [SLOTS, 2, 2, W])
        a_den = sb("a_den", [BUCKET, 2, 2, HEADS])
        a_inv = sb("a_inv", [BUCKET, 2, 2, HEADS])
        a_mean = sb("a_mean", [BUCKET, 2, 2, D])
        a_out = sb("a_out", [BUCKET, DEEP, 2, D])

        g_zero = sb("g_zero", [LANES, 20 * W])
        g_idx = sb("g_idx", [LANES, 2], I32)
        g_x = sb("g_x", [LANES, 2, D])
        g_acc = sb("g_acc", [LANES, W])
        g_stats = sb("g_stats", [LANES, 2, 6])
        g_mv = sb("g_mv", [LANES, 2, 2])
        g_rstd = sb("g_rstd", [LANES, 2, 2])
        g_hT = sb("g_hT", [128, 2, LANES])
        g_att = sb("g_att", [LANES, 2, HEADS])
        g_prod = sb("g_prod", [LANES, D])
        g_q = sb("g_q", [LANES, D])
        g_res = sb("g_res", [LANES, W])
        g_sb = sb("g_sb", [LANES, LANES])
        g_sel = sb("g_sel", [LANES, LANES])
        g_cnt = sb("g_cnt", [LANES, 1])
        g_to = sb("g_to", [LANES, 1], I32)
        g_new = sb("g_new", [LANES, W])
        f_acc = sb("f_acc", [LANES, RB, W])
        f_x = sb("f_x", [LANES, RB, D])
        f_r = sb("f_r", [LANES, RB, HEADS])
        f_o = sb("f_o", [LANES, RB, D])

        bank = [psum(f"bank{n}", [128, 512]) for n in range(8)]
        p_T, p_S, p_qkv, p_agg = bank[0:4]
        p_count, p_hT, p_q = bank[0:2], bank[2:4], bank[4:6]
        p_kv, p_aT, p_qe, p_sum = bank[0:4], bank[4:6], bank[6], bank[7]

        s_in = sem("s_in")
        s_passed = sem("s_passed")
        s_const = sem("s_const")
        s_masks = sem("s_masks")
        s_srcf = sem("s_srcf")
        s_cleared = sem("s_cleared")
        s_iota = sem("s_iota")
        s_zero = sem("s_zero")
        s_qpad = sem("s_qpad")
        s_setup = sem("s_setup")
        s_ready = sem("s_ready")
        se_hot = sem("se_hot")
        se_seen = sem("se_seen")
        se_counted = sem("se_counted")
        se_free = sem("se_free")
        se_count = sem("se_count")
        se_field = sem("se_field")
        se_rank = sem("se_rank")
        se_over = sem("se_over")
        se_in = sem("se_in")
        se_off = sem("se_off")
        se_slot = sem("se_slot")
        se_pay = sem("se_pay")
        sn_stats = sem("sn_stats")
        sn_mv = sem("sn_mv")
        sn_ln = sem("sn_ln")
        sn_rstd = sem("sn_rstd")
        sn_bias = sem("sn_bias")
        sn_h = sem("sn_h")
        sn_hT = sem("sn_hT")
        sn_hTc = sem("sn_hTc")
        sn_q = sem("sn_q")
        sn_qc = sem("sn_qc")
        s_over = sem("s_over")
        s_osum = sem("s_osum")
        s_left = sem("s_left")
        s_slots = sem("s_slots")
        s_slotf = sem("s_slotf")
        s_slotT = sem("s_slotT")
        s_dec = sem("s_dec")
        s_dst = sem("s_dst")
        sa_idx = sem("sa_idx")
        sa_hot = sem("sa_hot")
        sa_T = sem("sa_T")
        sa_Tc = sem("sa_Tc")
        sa_kv = sem("sa_kv")
        sa_qe = sem("sa_qe")
        sa_qc = sem("sa_qc")
        sa_prod = sem("sa_prod")
        sa_att = sem("sa_att")
        sa_clip = sem("sa_clip")
        sa_exp = sem("sa_exp")
        sa_res = sem("sa_res")
        sa_sum = sem("sa_sum")
        sa_off = sem("sa_off")
        sa_den = sem("sa_den")
        sa_inv = sem("sa_inv")
        sa_mean = sem("sa_mean")
        sa_out = sem("sa_out")
        se_put = [sem(f"se_put{b}") for b in range(GB)]
        sn_x = [sem(f"sn_x{b}") for b in range(GB)]
        sn_hout = [sem(f"sn_hout{b}") for b in range(GB)]
        sn_qout = [sem(f"sn_qout{b}") for b in range(GB)]
        sa_h = [sem(f"sa_h{b}") for b in range(DEEP)]
        sa_q = [sem(f"sa_q{b}") for b in range(DEEP)]
        sa_x = [sem(f"sa_x{b}") for b in range(DEEP)]
        sa_store = [sem(f"sa_store{b}") for b in range(DEEP)]
        sg_zero = sem("sg_zero")
        sg_cleared = sem("sg_cleared")
        sg_idx = sem("sg_idx")
        sg_gathered = sem("sg_gathered")
        sg_scattered = sem("sg_scattered")
        sg_stats = sem("sg_stats")
        sg_mv = sem("sg_mv")
        sg_ln = sem("sg_ln")
        sg_rstd = sem("sg_rstd")
        sg_norm = sem("sg_norm")
        sg_xT = sem("sg_xT")
        sg_hT = sem("sg_hT")
        sg_qkv = sem("sg_qkv")
        sg_q = sem("sg_q")
        sg_sb = sem("sg_sb")
        sg_sT = sem("sg_sT")
        sg_sel = sem("sg_sel")
        sg_cnt = sem("sg_cnt")
        sg_far = sem("sg_far")
        sg_to = sem("sg_to")
        sg_prod = sem("sg_prod")
        sg_att = sem("sg_att")
        sg_clip = sem("sg_clip")
        sg_exp = sem("sg_exp")
        sg_res = sem("sg_res")
        sg_agg = sem("sg_agg")
        sg_new = sem("sg_new")
        sf_done = sem("sf_done")
        sf_in = sem("sf_in")
        sf_r = sem("sf_r")
        sf_o = sem("sf_o")
        sf_out = sem("sf_out")

        block = ctx.enter_context(nc.Block())

        def hold(eng, semaphore, value):
            eng.wait_ge(semaphore, value)
            eng.sem_inc(s_passed, 1)

        def general_sync(sp):
            sp.wait_ge(sg_zero, 1)
            with sp.Fori(0, T // 20) as i:
                sp.dma_start(acc_lanes[:, bass.ds(i * (20 * W), 20 * W)], g_zero[:]).then_inc(sg_cleared, 16)
            sp.wait_ge(sf_done, 1)
            with sp.Fori(0, ROWS // RB) as i:
                sp.dma_start(f_acc[:].rearrange("p t w -> p (t w)"),
                             acc_lanes[:, bass.ds(i * (RB * W), RB * W)]).then_inc(sf_in, 16)
                sp.dma_start(f_x[:].rearrange("p t d -> p (t d)"),
                             x_lanes[:, bass.ds(i * (RB * D), RB * D)]).then_inc(sf_in, 16)
                sp.wait_ge(sf_o, 2 * i + 2)
                sp.dma_start(out_lanes[:, bass.ds(i * (RB * D), RB * D)],
                             f_o[:].rearrange("p t d -> p (t d)")).then_inc(sf_out, 16)
                hold(sp, sf_out, 16 * i + 16)

        def general_pool(pool):
            pool.wait_ge(sg_cleared, 16 * (T // 20))
            with pool.Fori(0, T) as i:
                pool.tensor_copy(g_idx[:, 0:1], src_i[:, bass.ds(i, 1)]).then_inc(sg_idx, 1)
                pool.tensor_copy(g_idx[:, 1:2], dst_i[:, bass.ds(i, 1)]).then_inc(sg_idx, 1)
                hold(pool, sg_idx, 2 * i + 2)
                at_src = bass.IndirectOffsetOnAxis(ap=g_idx[:, 0:1], axis=0)
                at_dst = bass.IndirectOffsetOnAxis(ap=g_idx[:, 1:2], axis=0)
                pool.indirect_dma_start(g_x[:, 0, :], None, x, at_src).then_inc(sg_gathered, 16)
                pool.indirect_dma_start(g_x[:, 1, :], None, x, at_dst).then_inc(sg_gathered, 16)
                pool.indirect_dma_start(g_acc[:], None, acc, at_src).then_inc(sg_gathered, 16)
                pool.wait_ge(sg_to, i + 1)
                hold(pool, sg_new, i + 1)
                pool.indirect_dma_start(acc, bass.IndirectOffsetOnAxis(ap=g_to[:, 0:1], axis=0), g_new[:], None,
                                        bounds_check=N - 1, oob_is_err=False).then_inc(sg_scattered, 16)
                hold(pool, sg_scattered, 16 * i + 16)
            pool.nop().then_inc(sf_done, 1)

        def general_vector(dve):
            dve.memset(g_zero[:], 0.0).then_inc(sg_zero, 1)
            with dve.Fori(0, T) as i:
                dve.tensor_copy(g_sb[:], src_f[:, bass.ds(i, 1)].to_broadcast([LANES, LANES])).then_inc(sg_sb, 1)
                dve.wait_ge(sg_gathered, 48 * i + 48)
                for k in range(2):
                    dve.bn_stats(g_stats[:, k, :], g_x[:, k, :]).then_inc(sg_stats, 1)
                hold(dve, sg_stats, 2 * i + 2)
                for k in range(2):
                    dve.bn_aggr(g_mv[:, k, :], g_stats[:, k, :]).then_inc(sg_mv, 1)
                dve.wait_ge(sg_sT, i + 1)
                dve.tensor_scalar(g_sel[:], p_S[0:LANES, 0:LANES], g_sb[:, 0:1], None,
                                  ALU.is_equal).then_inc(sg_sel, 1)
                dve.wait_ge(sg_sel, i + 1)
                dve.tensor_tensor_reduce(g_prod[:, 0:LANES], g_sel[:], before[0:LANES, 0:LANES], 1.0, 0.0, ALU.mult,
                                         ALU.add, g_cnt[:]).then_inc(sg_cnt, 1)
                dve.wait_ge(sg_cnt, i + 1)
                dve.scalar_tensor_tensor(g_to[:], g_cnt[:], float(FAR), g_sb[:, 0:1], ALU.mult,
                                         ALU.add).then_inc(sg_to, 1)
                dve.wait_ge(sg_rstd, i + 1)
                for k in range(2):
                    dve.tensor_scalar(g_x[:, k, :], g_x[:, k, :], g_mv[:, k, 0:1], g_rstd[:, 1, k:k + 1],
                                      ALU.subtract, ALU.mult).then_inc(sg_norm, 1)
                dve.wait_ge(sg_q, i + 1)
                dve.tensor_tensor(g_prod[:], g_q[:], p_qkv[0:LANES, D:2 * D],
                                  ALU.mult).then_inc(sg_prod, 1)
                dve.wait_ge(sg_prod, i + 1)
                dve.tensor_reduce(g_att[:, 0, :], g_prod[:].rearrange("p (h d) -> p h d", h=HEADS), AX_X,
                                  ALU.add).then_inc(sg_att, 1)
                dve.wait_ge(sg_att, i + 1)
                dve.tensor_scalar(g_att[:, 1, :], g_att[:, 0, :], -CLIP, CLIP, ALU.max, ALU.min).then_inc(sg_clip, 1)
                dve.wait_ge(sg_exp, i + 1)
                dve.tensor_tensor(g_res[:, 0:D].rearrange("p (h d) -> p h d", h=HEADS),
                                  p_qkv[0:LANES, 2 * D:3 * D].rearrange("p (h d) -> p h d", h=HEADS),
                                  g_res[:, D:W].unsqueeze(2).to_broadcast([LANES, HEADS, HD]),
                                  ALU.mult).then_inc(sg_res, 1)
                dve.wait_ge(sg_agg, i + 1)
                dve.tensor_tensor(g_new[:], p_agg[0:LANES, 0:W], g_acc[:], ALU.add).then_inc(sg_new, 1)
            with dve.Fori(0, ROWS // RB) as i:
                dve.wait_ge(sf_in, 32 * i + 32)
                dve.tensor_scalar(f_r[:], f_acc[:, :, D:W], NORM_EPS, None, ALU.add).then_inc(sf_r, 1)
                dve.wait_ge(sf_r, 2 * i + 1)
                dve.reciprocal(f_r[:], f_r[:]).then_inc(sf_r, 1)
                dve.wait_ge(sf_r, 2 * i + 2)
                for t in range(RB):
                    last = dve.tensor_tensor(f_o[:, t, :].rearrange("p (h d) -> p h d", h=HEADS),
                                             f_acc[:, t, 0:D].rearrange("p (h d) -> p h d", h=HEADS),
                                             f_r[:, t, :].unsqueeze(2).to_broadcast([LANES, HEADS, HD]), ALU.mult)
                last.then_inc(sf_o, 1)
                dve.wait_ge(sf_o, 2 * i + 1)
                dve.tensor_tensor(f_o[:], f_o[:], f_x[:], ALU.add).then_inc(sf_o, 1)

        def general_scalar(act):
            with act.Fori(0, T) as i:
                act.wait_ge(sg_mv, 2 * i + 2)
                act.activation(g_rstd[:, 0, :], g_mv[:, :, 1], ACT.Ln, bias=eps_col[0:LANES, :]).then_inc(sg_ln, 1)
                act.wait_ge(sg_ln, i + 1)
                act.activation(g_rstd[:, 1, :], g_rstd[:, 0, :], ACT.Exp, scale=-0.5).then_inc(sg_rstd, 1)
                act.wait_ge(sg_xT, i + 1)
                act.activation(g_hT[:], p_T[:, 0:2 * LANES].rearrange("p (k l) -> p k l", k=2),
                               ACT.Relu).then_inc(sg_hT, 1)
                act.wait_ge(sg_qkv, i + 1)
                act.activation(g_q[:], p_qkv[0:LANES, 0:D], ACT.Copy).then_inc(sg_q, 1)
                act.wait_ge(sg_clip, i + 1)
                act.activation(g_res[:, D:W], g_att[:, 1, :], ACT.Exp).then_inc(sg_exp, 1)

        def general_tensor(pe):
            with pe.Fori(0, T) as i:
                pe.wait_ge(sg_sb, i + 1)
                pe.transpose(p_S[0:LANES, 0:LANES], g_sb[:], ident[0:LANES, 0:LANES]).then_inc(sg_sT, 1)
                pe.wait_ge(sg_norm, 2 * i + 2)
                for k in range(2):
                    last = pe.transpose(p_T[:, k * LANES:(k + 1) * LANES], g_x[:, k, :], ident[0:LANES, 0:LANES])
                last.then_inc(sg_xT, 1)
                pe.wait_ge(sg_hT, i + 1)
                pe.matmul(p_qkv[0:LANES, 0:D], g_hT[:, 0, :], q_w[:], start=True, stop=True)
                pe.matmul(p_qkv[0:LANES, D:3 * D], g_hT[:, 1, :], kv_w[:], start=True, stop=True).then_inc(sg_qkv, 1)
                pe.wait_ge(sg_res, i + 1)
                pe.wait_ge(sg_sel, i + 1)
                pe.matmul(p_agg[0:LANES, 0:W], g_sel[:], g_res[:], start=True, stop=True).then_inc(sg_agg, 1)

        def need(eng, semaphore, value):
            if not isinstance(value, int) or value > 0:
                eng.wait_ge(semaphore, value)

        def steps(eng, step, first, lo, hi, last, period):
            for k in range(first, lo):
                step(k // period, k % period)
            with eng.Fori(lo // period, hi // period) as m:
                for b in range(period):
                    step(m, b)
            for k in range(hi, last):
                step(k // period, k % period)

        def later(m, b, by, period):
            q, r = divmod(b + by, period)
            return m + q, r, period * (m + q) + r

        def there(k, count):
            return not isinstance(k, int) or 0 <= k < count

        def node_rows(dram, g, parts):
            return dram[bass.ds(g * GN, parts * EG)].rearrange("(p r) d -> p r d", r=EG)

        def parts_of(g):
            return LAST if isinstance(g, int) and g == ND else 128

        def groups(eng, step, first=0, last=NG):
            steps(eng, step, first, GB, ND - GB, last, GB)

        def sort_sync(sp):
            def load(m, b, g):
                if there(g, ND + 1):
                    need(sp, sn_h, EG * (g - GB + 1))
                    parts = parts_of(g)
                    sp.dma_start(n_x[0:parts, b], node_rows(x, g, parts)).then_inc(sn_x[b], 16)

            def step(m, b):
                load(*later(m, b, 1, GB))
                m, b, g = later(m, b, -1, GB)
                if there(g, ND + 1):
                    parts = parts_of(g)
                    sp.wait_ge(sn_h, EG * g + EG)
                    sp.dma_start(node_rows(h_dram, g, parts), n_h[0:parts, b]).then_inc(sn_hout[b], 16)
                m, b, g = later(m, b, -1, GB)
                if there(g, ND + 1):
                    parts = parts_of(g)
                    sp.wait_ge(sn_qc, 2 * g + 2)
                    sp.dma_start(node_rows(q_dram, g, parts), n_q[0:parts, b]).then_inc(sn_qout[b], 16)
            load(0, 0, 0)
            groups(sp, step, last=NG + 1)

        def sort_pool(pool):
            pool.wait_ge(s_cleared, 16)
            def step(m, b):
                g = GB * m + b
                hold(pool, se_slot, g + 1)
                for j in range(EG):
                    pool.indirect_dma_start(slots, bass.IndirectOffsetOnAxis(ap=e_slot[:, b, j:j + 1], axis=0),
                                            e_pay[:, b, j:j + 1], None,
                                            bounds_check=2 * NB * SLOTS - 1, oob_is_err=False).then_inc(se_put[b], 16)
            groups(pool, step)

        def sort_vector(dve):
            def hot(t, j):
                need(dve, se_free, t - NHOT + 1)
                dve.tensor_scalar(e_hot[:, j % NHOT, :], iota_b[:], col_f[:, bass.ds(t, 1)], unit_f[:, bass.ds(t, 1)],
                                  ALU.is_equal, ALU.mult).then_inc(se_hot, 1)

            def slot_of(m, b, g, part):
                at = bass.ds(EG * g, EG)
                if part == 1:
                    dve.wait_ge(se_seen, EG * g + EG)
                    dve.tensor_tensor(e_count[:, b, :], e_raw[:, b, :], inv_f[:, at], ALU.mult).then_inc(se_count, 1)
                if part == 2:
                    dve.wait_ge(se_count, g + 1)
                    dve.tensor_tensor(e_field[:, b, :], e_count[:, b, :], shift_i[:, at],
                                      ALU.logical_shift_right).then_inc(se_field, 1)
                if part == 3:
                    dve.wait_ge(se_field, g + 1)
                    dve.tensor_scalar(e_rank[:, b, :], e_field[:, b, :], 255, None, ALU.bitwise_and).then_inc(se_rank, 1)
                if part == 4:
                    dve.wait_ge(se_rank, g + 1)
                    dve.tensor_tensor(e_off[:, b, :], e_rank[:, b, :], sign[:], ALU.mult).then_inc(se_off, 1)
                    dve.tensor_scalar(over_f[:, at], e_rank[:, b, :], float(SLOTS), FAR_SLOT, ALU.is_ge,
                                      ALU.mult).then_inc(se_over, 1)
                if part == 5:
                    dve.wait_ge(se_off, g + 1)
                    dve.tensor_tensor(e_in[:, b, :], e_off[:, b, :], first_f[:, at], ALU.add).then_inc(se_in, 1)
                if part == 6:
                    need(dve, se_put[b], 16 * EG * m)
                    dve.wait_ge(se_over, g + 1)
                    dve.wait_ge(se_in, g + 1)
                    dve.wait_ge(se_pay, g + 1)
                    dve.tensor_tensor(e_slot[:, b, :], e_in[:, b, :], over_f[:, at], ALU.add).then_inc(se_slot, 1)

            def step(m, b):
                g = GB * m + b
                m_p, b_p, g_p = later(m, b, -1, GB)
                for j in range(EG):
                    t = EG * g + j
                    if there(t + 1, T):
                        hot(t + 1, j + 1)
                    if there(g, ND + 1):
                        parts = parts_of(g)
                        if j == 0:
                            dve.wait_ge(sn_x[b], 16 * m + 16)
                        dve.bn_stats(n_stats[0:parts, b, j, :], n_x[0:parts, b, j, :]).then_inc(sn_stats, 1)
                    if there(g_p, ND + 1):
                        parts = parts_of(g_p)
                        if j == 1:
                            hold(dve, sn_stats, EG * g_p + EG)
                            for i in range(EG):
                                dve.bn_aggr(n_mv[0:parts, b_p, i, :], n_stats[0:parts, b_p, i, :]).then_inc(sn_mv, 1)
                        if j == 4:
                            dve.wait_ge(sn_rstd, g_p + 1)
                            dve.scalar_tensor_tensor(n_bias[0:parts, b_p, :], n_mv[0:parts, b_p, :, 0], -1.0,
                                                     n_rstd[0:parts, b_p, :], ALU.mult, ALU.mult).then_inc(sn_bias, 1)
                    if there(g_p, NG):
                        slot_of(m_p, b_p, g_p, j)
                    if there(t, T):
                        need(dve, se_seen, t)
                        dve.wait_ge(se_counted, t + 1)
                        dve.tensor_tensor_reduce(e_skip[:], p_count[j % 2][0:LANES, 0:COLS], e_hot[:, j % NHOT, :], 1.0,
                                                 0.0, ALU.mult, ALU.add, e_raw[:, b, j:j + 1]).then_inc(se_seen, 1)
            hot(0, 0)
            groups(dve, step, last=NG + 1)

        def sort_scalar(act):
            def step(m, b):
                g = GB * m + b
                if there(g, NG):
                    need(act, se_put[b], 16 * EG * m)
                    act.activation(e_pay[:, b, :], pay_f[:, bass.ds(EG * g, EG)], ACT.Copy).then_inc(se_pay, 1)
                m1, b1, g1 = later(m, b, -1, GB)
                m2, b2, g2 = later(m, b, -2, GB)
                if there(g1, ND + 1):
                    parts = parts_of(g1)
                    act.wait_ge(sn_mv, EG * g1 + EG)
                    act.activation(n_ln[0:parts, b1, :], n_mv[0:parts, b1, :, 1], ACT.Ln,
                                   bias=eps_col[0:parts, :]).then_inc(sn_ln, 1)
                    act.wait_ge(sn_ln, g1 + 1)
                    act.activation(n_rstd[0:parts, b1, :], n_ln[0:parts, b1, :], ACT.Exp,
                                   scale=-0.5).then_inc(sn_rstd, 1)
                if there(g2, ND + 1):
                    parts = parts_of(g2)
                    for s in range(2):
                        need(act, sn_q, 2 * g2 + s - 1)
                        act.wait_ge(sn_hT, 2 * g2 + s + 1)
                        act.activation(n_hT[:, s, 0:4 * parts], p_hT[s][:, 0:4 * parts], ACT.Copy).then_inc(sn_hTc, 1)
                if there(g1, ND + 1):
                    parts = parts_of(g1)
                    need(act, sn_hout[b1], 16 * m1)
                    act.wait_ge(sn_bias, g1 + 1)
                    for j in range(EG):
                        act.activation(n_h[0:parts, b1, j, :], n_x[0:parts, b1, j, :], ACT.Relu,
                                       bias=n_bias[0:parts, b1, j:j + 1],
                                       scale=n_rstd[0:parts, b1, j:j + 1]).then_inc(sn_h, 1)
                if there(g2, ND + 1):
                    parts = parts_of(g2)
                    need(act, sn_qout[b2], 16 * m2)
                    for s in range(2):
                        act.wait_ge(sn_q, 2 * g2 + s + 1)
                        act.activation(n_q[0:parts, b2, 4 * s:4 * s + 4, :],
                                       p_q[s][0:parts, :].rearrange("p (r d) -> p r d", d=D),
                                       ACT.Copy).then_inc(sn_qc, 1)
            groups(act, step, last=NG + 1)

        def sort_tensor(pe):
            def count(t, j, part, wait_for, to_signal):
                pe.wait_ge(*wait_for)
                pe.matmul(p_count[j % 2][0:LANES, 0:COLS], upto[:, part, :], e_hot[:, j % NHOT, :], start=False,
                          stop=True, skip_group_check=True).then_inc(to_signal, 1)

            def step(m, b):
                g = GB * m + b
                m2, b2, g2 = later(m, b, -2, GB)
                dense = there(g2, ND + 1)
                parts = parts_of(g2)
                for j in range(EG):
                    t = EG * g + j
                    if there(t + 1, T):
                        count(t + 1, j + 1, 0, (se_hot, t + 2), se_counted)
                    if dense and j in (1, 2):
                        s = j - 1
                        need(pe, sn_hTc, 2 * g2 + s - 1)
                        pe.wait_ge(sn_h, EG * g2 + 4 * s + 4)
                        for i in range(4):
                            last = pe.transpose(p_hT[s][:, i * parts:(i + 1) * parts], n_h[0:parts, b2, 4 * s + i, :],
                                                ident[0:parts, 0:parts])
                        last.then_inc(sn_hT, 1)
                    if dense and j >= 4:
                        s = (j - 4) // 2
                        if j % 2 == 0:
                            need(pe, sn_qc, 2 * g2 + s - 1)
                            pe.wait_ge(sn_hTc, 2 * g2 + s + 1)
                        for i in range(j % 2 * 2, j % 2 * 2 + 2):
                            last = pe.matmul(p_q[s][0:parts, i * D:(i + 1) * D], n_hT[:, s, i * parts:(i + 1) * parts],
                                             q_w[:], start=True, stop=True)
                        if j % 2:
                            last.then_inc(sn_q, 1)
                    if there(t, T):
                        count(t, j, 1, (se_seen, t + 1), se_free)

            for c in range(2):
                pe.matmul(p_count[c][0:LANES, 0:COLS], upto[:, 0, :], zero_h[:], start=True, stop=True)
            count(0, 0, 0, (se_hot, 1), se_counted)
            groups(pe, step, last=NG + 1)

        def attend(eng, step, first=0, last=NP):
            steps(eng, step, first, DEEP, NP - DEEP, last, DEEP)

        def two_buckets(dram, k):
            return dram[bass.ds(k * 2 * BUCKET, 2 * BUCKET)].rearrange("(j n) d -> n j d", j=2)

        def attend_sync(sp):
            sp.dma_start(slot_i[:], slot_rows).then_inc(s_slots, 16)

            def step(m, b):
                mq, bq, kq = later(m, b, 5, DEEP)
                if there(kq, NP):
                    need(sp, sa_qe, kq - DEEP + 1)
                    sp.dma_start(a_q[:, bq], two_buckets(q_dram, kq)).then_inc(sa_q[bq], 16)
                mx, bx, kx = later(m, b, 2, DEEP)
                if there(kx, NP):
                    need(sp, sa_out, kx - DEEP + 1)
                    if isinstance(kx, int) and kx == NP - 1:
                        sp.dma_start(a_x[0:TAIL, bx, 0, :], x[N - TAIL:N]).then_inc(sa_x[bx], 16)
                    else:
                        sp.dma_start(a_x[:, bx], two_buckets(x, kx)).then_inc(sa_x[bx], 16)
                mo, bo, ko = later(m, b, -2, DEEP)
                if there(ko, NP):
                    sp.wait_ge(sa_out, ko + 1)
                    if isinstance(ko, int) and ko == NP - 1:
                        sp.dma_start(out[N - TAIL:N], a_out[0:TAIL, bo, 0, :]).then_inc(sa_store[bo], 16)
                    else:
                        sp.dma_start(two_buckets(out, ko), a_out[:, bo]).then_inc(sa_store[bo], 16)
            attend(sp, step, first=-5, last=NP + 2)
            for b in range(DEEP):
                sp.wait_ge(sa_store[b], 16 * (NP // DEEP))

        def attend_pool(pool):
            for b in range(GB):
                pool.wait_ge(sn_hout[b], 16 * len(range(b, ND + 1, GB)))

            def step(m, b):
                k = DEEP * m + b
                hold(pool, sa_idx, k + 1)
                for j in range(2):
                    pool.indirect_dma_start(a_h[:, b, j, :], None, h_dram,
                                            bass.IndirectOffsetOnAxis(ap=a_idx[:, b, j:j + 1], axis=0)
                                            ).then_inc(sa_h[b], 16)
            attend(pool, step)

        def attend_vector(dve):
            dve.wait_ge(s_slots, 16)
            dve.tensor_tensor(slot_f[:], slot_i[:, 0:NB // 128], slot_i[:, NB // 128:], ALU.add).then_inc(s_slotf, 1)
            dve.wait_ge(s_slotT, 1)
            dve.tensor_copy(pay_i[:], bank[6][:, 0:NB]).then_inc(s_dec, 1)
            dve.wait_ge(s_dec, 1)
            dve.tensor_scalar(dst_col[:], pay_i[:], 7, None, ALU.logical_shift_right).then_inc(s_dst, 1)
            dve.tensor_scalar(place_i[:], pay_i[:], 127, None, ALU.bitwise_and).then_inc(s_dec, 1)
            dve.wait_ge(s_dec, 2)
            dve.tensor_copy(place_col[:], place_i[:]).then_inc(s_dec, 1)
            dve.wait_ge(s_dec, 3)

            def step(m, b):
                k, c = DEEP * m + b, b % 2
                mp, bp, kp = later(m, b, -1, DEEP)
                cp = bp % 2
                now, before_ = there(k, NP), there(kp, NP)
                heads = "p j (h d) -> p (j h) d"
                if now:
                    dve.wait_ge(sa_kv, k + 1)
                    dve.wait_ge(sa_qc, k + 1)
                    dve.tensor_tensor(a_prod[:, c], p_kv[b % 4][:].rearrange("p (j w) -> p j w", j=2)[:, :, 0:D],
                                      a_qe[:, c], ALU.mult).then_inc(sa_prod, 1)
                p_prev = p_sum[0:BUCKET, 0:2 * W].rearrange("p (j w) -> p j w", j=2)
                mo, bo, ko = later(m, b, -2, DEEP)
                if there(ko, NP):
                    dve.wait_ge(sa_x[bo], 16 * mo + 16)
                    need(dve, sa_store[bo], 16 * mo)
                    dve.wait_ge(sa_mean, ko + 1)
                    dve.tensor_tensor(a_out[:, bo], a_mean[:, c], a_x[:, bo], ALU.add).then_inc(sa_out, 1)
                if now:
                    dve.wait_ge(sa_prod, k + 1)
                    dve.tensor_reduce(a_att[:, c].rearrange("p j h -> p (j h)"), a_prod[:, c].rearrange("p j (h d) -> p (j h) d", h=HEADS),
                                      AX_X, ALU.add).then_inc(sa_att, 1)
                if before_:
                    dve.wait_ge(sa_sum, kp + 1)
                    dve.tensor_scalar(a_den[:, cp], p_prev[:, :, D:W], NORM_EPS, None, ALU.add).then_inc(sa_den, 1)
                if now:
                    dve.wait_ge(sa_att, k + 1)
                    dve.tensor_scalar(a_clip[:, c], a_att[:, c], -CLIP, CLIP, ALU.max, ALU.min).then_inc(sa_clip, 1)
                if before_:
                    dve.wait_ge(sa_den, kp + 1)
                    dve.reciprocal(a_inv[:, cp], a_den[:, cp]).then_inc(sa_inv, 1)
                    dve.wait_ge(sa_inv, kp + 1)
                    dve.tensor_tensor(a_mean[:, cp].rearrange("p j (h d) -> p j h d", h=HEADS),
                                      p_prev[:, :, 0:D].rearrange("p j (h d) -> p j h d", h=HEADS),
                                      a_inv[:, cp].unsqueeze(3).to_broadcast([BUCKET, 2, HEADS, HD]),
                                      ALU.mult).then_inc(sa_mean, 1)
                if now:
                    dve.wait_ge(sa_exp, k + 1)
                    dve.tensor_tensor(a_res[:, c, :, 0:D].rearrange("p j (h d) -> p j h d", h=HEADS),
                                      p_kv[b % 4][:].rearrange("p (j w) -> p j w", j=2)[:, :, D:2 * D]
                                      .rearrange("p j (h d) -> p j h d", h=HEADS),
                                      a_res[:, c, :, D:W].unsqueeze(3).to_broadcast([SLOTS, 2, HEADS, HD]),
                                      ALU.mult).then_inc(sa_res, 1)
            attend(dve, step, last=NP + 2)

        def attend_scalar(act):
            act.wait_ge(s_dst, 1)
            act.wait_ge(s_dec, 3)

            def step(m, b):
                k = DEEP * m + b
                if there(k, NP):
                    need(act, sa_sum, k - 1)
                    act.wait_ge(sa_clip, k + 1)
                    act.activation(a_res[:, b % 2, :, D:W], a_clip[:, b % 2], ACT.Exp).then_inc(sa_exp, 1)
                mq, bq, kq = later(m, b, 2, DEEP)
                if there(kq, NP):
                    need(act, sa_prod, kq - 1)
                    act.wait_ge(sa_qe, kq + 1)
                    act.activation(a_qe[:, bq % 2], p_qe[:, 0:2 * D].rearrange("p (j d) -> p j d", j=2),
                                   ACT.Copy).then_inc(sa_qc, 1)
                mh, bh, kh = later(m, b, 3, DEEP)
                if there(kh, NP):
                    need(act, sa_kv, kh - 1)
                    act.wait_ge(sa_T, kh + 1)
                    act.activation(a_T[:, bh % 2].rearrange("p a b -> p (a b)"), p_aT[bh % 2][:],
                                   ACT.Copy).then_inc(sa_Tc, 1)
                mh, bh, kh = later(m, b, 4, DEEP)
                if there(kh, NP):
                    need(act, sa_hot, kh - 1)
                    for j in range(2):
                        act.activation(a_off[:, bh % 2, j, :], iota_f[:], ACT.Abs, scale=-1.0,
                                       bias=place_col[:, bass.ds(2 * kh + j, 1)]).then_inc(sa_off, 1)
                    need(act, sa_sum, kh - DEEP + 1)
                    act.wait_ge(sa_off, 2 * kh + 2)
                    act.activation(a_hot[:, bh].rearrange("p a b -> p (a b)"),
                                   a_off[:, bh % 2].rearrange("p a b -> p (a b)"), ACT.Relu, scale=-1.0,
                                   bias=one_col[:]).then_inc(sa_hot, 1)
                mi, bi, ki = later(m, b, 6, DEEP)
                if there(ki, NP):
                    need(act, sa_T, ki - DEEP + 1)
                    act.activation(a_idx[:, bi, :], dst_col[:, bass.ds(2 * ki, 2)], ACT.Copy).then_inc(sa_idx, 1)
            attend(act, step, first=-6)

        def attend_tensor(pe):
            pe.wait_ge(s_slotf, 1)
            for c in range(NB // 128):
                last = pe.transpose(bank[6][:, c * 128:(c + 1) * 128], slot_f[:, c, :], ident[:])
            last.then_inc(s_slotT, 1)

            def step(m, b):
                mp, bp, kp = later(m, b, -1, DEEP)
                if there(kp, NP):
                    c = bp % 2
                    need(pe, sa_mean, kp)
                    pe.wait_ge(sa_res, kp + 1)
                    for j in range(2):
                        last = pe.matmul(p_sum[0:BUCKET, j * W:(j + 1) * W], a_hot[:, bp, j, :],
                                         a_res[:, c, j, :], start=True, stop=True)
                    last.then_inc(sa_sum, 1)
                mq, bq, kq = later(m, b, 2, DEEP)
                if there(kq, NP):
                    c = bq % 2
                    need(pe, sa_qc, kq)
                    pe.wait_ge(sa_Tc, kq + 1)
                    pe.wait_ge(sa_q[bq], 16 * mq + 16)
                    for j in range(2):
                        last = pe.matmul(p_qe[:, j * D:(j + 1) * D], a_T[0:BUCKET, c, 2 + j, :], a_q[:, bq, j, :],
                                         start=True, stop=True)
                    last.then_inc(sa_qe, 1)
                mh, bh, kh = later(m, b, 3, DEEP)
                if there(kh, NP):
                    need(pe, sa_Tc, kh - 1)
                    pe.wait_ge(sa_h[bh], 32 * mh + 32)
                    for j in range(2):
                        pe.transpose(p_aT[bh % 2][:, j * 128:(j + 1) * 128], a_h[:, bh, j, :], ident[:])
                    pe.wait_ge(sa_hot, kh + 1)
                    for j in range(2):
                        last = pe.transpose(p_aT[bh % 2][0:BUCKET, (2 + j) * 128:(3 + j) * 128], a_hot[:, bh, j, :], ident[:])
                    last.then_inc(sa_T, 1)
                if there(kq, NP):
                    need(pe, sa_res, kq - 3)
                    for j in range(2):
                        last = pe.matmul(p_kv[bq % 4][:, j * 2 * D:(j + 1) * 2 * D], a_T[:, bq % 2, j, :], kv_w[:],
                                         start=True, stop=True)
                    last.then_inc(sa_kv, 1)
            attend(pe, step, first=-3, last=NP + 1)

        def either(eng, general, fast):
            eng.wait_ge(s_over, 1)
            over = eng.value_load(over_i[0:1, 0:1], min_val=0, max_val=1)
            with eng.If(over > 0):
                general(eng)
            with eng.Else():
                fast(eng)

        @block.sync
        def _(sp):
            sp.dma_start(src_i[:], src_lanes).then_inc(s_in, 16)
            sp.dma_start(dst_i[:], dst_lanes).then_inc(s_in, 16)
            sp.dma_start(q_w[:], qW).then_inc(s_in, 16)
            sp.dma_start(kv_w[:, 0:D], kW).then_inc(s_in, 16)
            sp.dma_start(kv_w[:, D:2 * D], vW).then_inc(s_in, 16)
            sp.wait_ge(s_zero, 3)
            sp.dma_start(slot_rows, zero_i[:].rearrange("b (c s) -> b c s", s=SLOTS)).then_inc(s_cleared, 16)
            sp.dma_start(q_dram[N:NB * BUCKET], zero_q[0:(NB * BUCKET - N) // 2].rearrange("p (r d) -> p r d", r=2)
                         ).then_inc(s_qpad, 16)
            sort_sync(sp)
            sp.wait_ge(s_qpad, 16)
            for b in range(GB):
                sp.wait_ge(se_put[b], 16 * EG * len(range(b, NG, GB)))
                sp.wait_ge(sn_hout[b], 16 * len(range(b, ND + 1, GB)))
                sp.wait_ge(sn_qout[b], 16 * len(range(b, ND + 1, GB)))
            either(sp, general_sync, attend_sync)

        @block.gpsimd
        def _(pool):
            pool.memset(ident[:], 1.0).then_inc(s_const, 1)
            pool.memset(before[:], 1.0).then_inc(s_const, 1)
            pool.memset(upto_f[:], 1.0).then_inc(s_const, 1)
            pool.wait_ge(s_const, 3)
            pool.affine_select(out=ident[:], in_=ident[:], compare_op=ALU.is_equal, fill=0.0, base=0,
                               pattern=[[-1, 128]], channel_multiplier=1).then_inc(s_masks, 1)
            pool.affine_select(out=before[:], in_=before[:], compare_op=ALU.is_gt, fill=0.0, base=0,
                               pattern=[[-1, 128]], channel_multiplier=1).then_inc(s_masks, 1)
            pool.affine_select(out=upto_f[:, 0, :], in_=upto_f[:, 0, :], compare_op=ALU.is_gt, fill=0.0, base=0,
                               pattern=[[1, LANES]], channel_multiplier=-1).then_inc(s_masks, 1)
            pool.affine_select(out=upto_f[:, 1, :], in_=upto_f[:, 1, :], compare_op=ALU.is_ge, fill=0.0, base=0,
                               pattern=[[-1, LANES]], channel_multiplier=1).then_inc(s_masks, 1)
            pool.iota(iota_i[:], pattern=[[1, NB]], base=0, channel_multiplier=0).then_inc(s_iota, 1)
            pool.wait_ge(s_masks, 4)
            sort_pool(pool)
            either(pool, general_pool, attend_pool)

        @block.vector
        def _(dve):
            def then(ins):
                chained[0] += 1
                ins.then_inc(s_setup, 1)
                dve.wait_ge(s_setup, chained[0])
            chained = [0]
            dve.memset(zero_i[:], 0).then_inc(s_zero, 1)
            dve.memset(zero_q[:], 0.0).then_inc(s_zero, 1)
            dve.memset(zero_h[:], 0.0).then_inc(s_zero, 1)
            dve.memset(eps_col[:], LN_EPS).then_inc(s_zero, 1)
            dve.memset(ones_f[:], 1.0).then_inc(s_zero, 1)
            dve.memset(one_col[:], 1.0).then_inc(s_zero, 1)
            dve.memset(sign[:], 1.0).then_inc(s_zero, 1)
            dve.wait_ge(s_zero, 7)
            then(dve.memset(sign[:].rearrange("p (t c) -> p t c", c=2)[:, :, 1:2], -1.0))
            dve.wait_ge(s_masks, 4)
            then(dve.tensor_copy(upto[:], upto_f[:]))
            dve.wait_ge(s_iota, 1)
            then(dve.tensor_copy(iota_b[:], iota_i[0:LANES, 0:COLS]))
            then(dve.tensor_scalar(iota_f[:], iota_i[:, 0:BUCKET], 1.0, None, ALU.add))
            dve.wait_ge(s_in, 80)
            then(dve.tensor_copy(src_f[:], src_i[:]))
            then(dve.tensor_scalar(bucket_i[:], src_f[:], 1.0 / BUCKET, None, ALU.mult))
            then(dve.tensor_copy(bucket_f[:], bucket_i[:]))
            then(dve.scalar_tensor_tensor(place_f[:], bucket_f[:], -float(BUCKET), src_f[:], ALU.mult, ALU.add))
            for op, step_ in ((ALU.is_lt, 1.0), (ALU.is_ge, -1.0)):
                then(dve.tensor_scalar(fix_f[:], place_f[:], 0.0 if step_ > 0 else float(BUCKET), None, op))
                then(dve.scalar_tensor_tensor(bucket_f[:], fix_f[:], -step_, bucket_f[:], ALU.mult, ALU.add))
                then(dve.scalar_tensor_tensor(place_f[:], fix_f[:], step_ * BUCKET, place_f[:], ALU.mult, ALU.add))
            then(dve.tensor_scalar(fix_f[:], bucket_f[:], float(COLS), None, ALU.is_ge))
            then(dve.tensor_scalar(col_f[:], bucket_f[:], 2.0 * COLS, None, ALU.is_ge))
            then(dve.tensor_scalar(unit_f[:], fix_f[:], 255.0, 1.0, ALU.mult, ALU.add))
            then(dve.scalar_tensor_tensor(unit_f[:], col_f[:], 65280.0, unit_f[:], ALU.mult, ALU.add))
            then(dve.tensor_tensor(fix_f[:], fix_f[:], col_f[:], ALU.add))
            then(dve.scalar_tensor_tensor(col_f[:], fix_f[:], -float(COLS), bucket_f[:], ALU.mult, ALU.add))
            then(dve.tensor_scalar(shift_i[:], fix_f[:], 8.0, None, ALU.mult))
            then(dve.tensor_scalar(inv_f[:], fix_f[:], 1.0, 255.0 / 256, ALU.min, ALU.mult))
            then(dve.tensor_scalar(fix_f[:], fix_f[:], -1.0, 0.0, ALU.add, ALU.max))
            then(dve.scalar_tensor_tensor(inv_f[:], fix_f[:], 255.0 / 65536, inv_f[:], ALU.mult, ALU.add))
            then(dve.tensor_scalar(inv_f[:], inv_f[:], -1.0, 1.0, ALU.mult, ALU.add))
            then(dve.tensor_copy(pay_f[:], dst_i[:]))
            then(dve.scalar_tensor_tensor(pay_f[:], pay_f[:], 128.0, place_f[:], ALU.mult, ALU.add))
            then(dve.tensor_scalar(pay_f[:], pay_f[:], 1.0, None, ALU.add))
            then(dve.tensor_scalar(first_f[:], bucket_f[:], float(SLOTS), None, ALU.mult))
            odd = first_f[:].rearrange("p (t c) -> p t c", c=2)[:, :, 1]
            then(dve.tensor_scalar(odd, odd, NB * SLOTS + SLOTS - 1.0, None, ALU.add))
            dve.nop().then_inc(s_ready, 1)
            sort_vector(dve)
            dve.wait_ge(se_free, T)
            dve.tensor_reduce(osum_f[:], over_f[:], AX_X, ALU.add).then_inc(s_osum, 1)
            for c in range(2):
                then(dve.tensor_copy(count_i[:, c, :], p_count[c][0:1, 0:COLS]))
            for f in range(FIELDS):
                then(dve.tensor_scalar(field_i[:, :, f, :], count_i[:], 8 * f, 255, ALU.logical_shift_right,
                                       ALU.bitwise_and))
            then(dve.tensor_tensor(count_f[:], field_i[:, 0].rearrange("p f c -> p (f c)"),
                                   field_i[:, 1].rearrange("p f c -> p (f c)"), ALU.add))
            then(dve.tensor_reduce(most_f[:], count_f[:], AX_X, ALU.max))
            then(dve.tensor_scalar(full_f[:], most_f[:], float(SLOTS), None, ALU.is_gt))
            dve.wait_ge(s_left, 1)
            then(dve.tensor_scalar(left_f[:], bank[6][0:1, 0:1], 0.0, None, ALU.is_gt))
            dve.tensor_tensor(over_i[:], full_f[:], left_f[:], ALU.max).then_inc(s_over, 1)
            either(dve, general_vector, attend_vector)

        @block.scalar
        def _(act):
            act.preload_act_table_set("natural_log_exp_and_others")
            act.wait_ge(s_ready, 1)
            sort_scalar(act)
            either(act, general_scalar, attend_scalar)

        @block.tensor
        def _(pe):
            pe.wait_ge(s_ready, 1)
            sort_tensor(pe)
            pe.wait_ge(s_osum, 1)
            pe.matmul(bank[6][0:1, 0:1], osum_f[:], ones_f[:], start=True, stop=True).then_inc(s_left, 1)
            pe.wait_ge(sn_hTc, 2 * (ND + 1))
            pe.wait_ge(sn_qc, 2 * (ND + 1))
            either(pe, general_tensor, attend_tensor)


def kernel(x, src, dst, L0_gnn_qW, L0_gnn_kW, L0_gnn_vW):
    import numpy as np
    import concourse.bacc as bacc
    from concourse.bass_utils import run_bass_kernel_spmd

    nc = bacc.Bacc("TRN2", target_bir_lowering=False, num_devices=1)
    given = {"x": x, "src": src, "dst": dst, "qW": L0_gnn_qW, "kW": L0_gnn_kW, "vW": L0_gnn_vW}
    arrays, aps = {}, {}
    for name, a in given.items():
        a = np.ascontiguousarray(a)
        arrays[f"in_{name}"] = a
        aps[name] = nc.dram_tensor(f"in_{name}", a.shape, mybir.dt.from_np(a.dtype), kind="ExternalInput").ap()
    out = nc.dram_tensor("out", list(x.shape), F32, kind="ExternalOutput").ap()
    gnn_kernel(nc, aps["x"], aps["src"], aps["dst"], aps["qW"], aps["kW"], aps["vW"], out)
    r = run_bass_kernel_spmd(nc, [arrays], core_ids=[0])
    return r.results[0]["out"]
```

```python
from contextlib import ExitStack

import concourse.bass as bass
from concourse import mybir

F32 = mybir.dt.float32
BF16 = mybir.dt.bfloat16
I32 = mybir.dt.int32
ALU = mybir.AluOpType
ACT = mybir.ActivationFunctionType
AX_X = mybir.AxisListType.X

LN_EPS = 1e-5
NORM_EPS = 1e-8
CLIP = 10.0
HEADS = 4
LANES = 125
EG = 8
BUCKET = 98
SLOTS = 128


def gnn_kernel(nc, x, src, dst, qW, kW, vW, out):
    N, D = x.shape
    E = src.shape[0]
    T = E // LANES
    HD = D // HEADS
    W = D + HEADS
    ROWS = N // LANES
    RB = 4
    FAR = 65536

    NB = 512
    NP = NB // 2
    NC = NB // 128
    PARTS = ((0, 1), (1, NC))
    DEEP = 8
    NHOT = 4
    FIELDS = 3
    COLS = -(-NB // FIELDS)
    GB = 3
    FAR_SLOT = float(2 * NB * SLOTS)
    NO_NODE = 1 << 20
    ROUND = 1.5 * (1 << 23)
    FULL = E // 128
    REST = E - 128 * FULL
    NG = -(-E // (128 * EG))
    ET = NG * EG
    GN = 128 * EG
    ND = N // GN
    LAST = (N - ND * GN) // EG
    TAIL = N - (NP - 1) * 2 * BUCKET
    assert N <= NB * BUCKET and 0 < TAIL <= BUCKET < 128 == SLOTS and NP % DEEP == 0
    assert 2 * SLOTS <= 256 and FIELDS * 8 <= 24 and 128 * N < 1 << 24
    assert ET % 2 == 0 and FULL < ET - 1 and REST > 0
    assert (N - ND * GN) % EG == 0 and ND <= NG <= ND + 1 and ND % GB == 0

    h_dram = nc.dram_tensor("h_rows", [N, D], F32, kind="Internal").ap()
    q_dram = nc.dram_tensor("q_rows", [NB * BUCKET, D], F32, kind="Internal").ap()
    slots = nc.dram_tensor("slots", [2 * NB * SLOTS, 1], I32, kind="Internal").ap()
    slot_rows = slots.rearrange("(c b s) o -> b c (s o)", b=128, s=SLOTS)
    acc = nc.dram_tensor("acc", [N, W], F32, kind="Internal").ap()
    src_lanes = src.rearrange("(p t) -> p t", p=LANES)
    dst_lanes = dst.rearrange("(p t) -> p t", p=LANES)
    acc_lanes = acc.rearrange("(p t) w -> p (t w)", p=LANES)
    x_lanes = x.rearrange("(p t) d -> p (t d)", p=LANES)
    out_lanes = out.rearrange("(p t) d -> p (t d)", p=LANES)

    with ExitStack() as ctx:
        def sb(name, shape, dt=F32):
            return ctx.enter_context(nc.sbuf_tensor(name, shape, dt))

        def psum(name, shape):
            return ctx.enter_context(nc.psum_tensor(name, shape, F32))

        def sem(name):
            return ctx.enter_context(nc.semaphore(name))

        ident = sb("ident", [128, 128])
        before = sb("before", [128, 128])
        q_w = sb("q_w", [128, D])
        kv_w = sb("kv_w", [128, 2 * D])
        eps_col = sb("eps_col", [128, 1])
        src_i = sb("src_i", [LANES, T], I32)
        dst_i = sb("dst_i", [LANES, T], I32)
        src_f = sb("src_f", [LANES, T])

        e_src = sb("e_src", [128, ET], I32)
        e_dst = sb("e_dst", [128, ET], I32)
        mid_f = sb("mid_f", [128, ET])
        bucket_f = sb("bucket_f", [128, ET])
        place_f = sb("place_f", [128, ET])
        last_f = sb("last_f", [128, ET])
        field_f = sb("field_f", [128, ET])
        unit_lin = sb("unit_lin", [128, ET])
        inv_lin = sb("inv_lin", [128, ET])
        first_f = sb("first_f", [128, ET])
        pay_f = sb("pay_f", [128, ET])
        iota_i = sb("iota_i", [128, COLS], I32)
        iota_b = sb("iota_b", [128, COLS], BF16)
        iota_f = sb("iota_f", [128, BUCKET])
        upto = sb("upto", [128, 2, 128], BF16)
        col_f = sb("col_f", [128, ET])
        unit_f = sb("unit_f", [128, ET])
        inv_f = sb("inv_f", [128, ET])
        shift_i = sb("shift_i", [128, ET], I32)
        all_ones = sb("all_ones", [128, 128])
        sign = sb("sign", [128, EG])
        e_hot = sb("e_hot", [128, NHOT, COLS], BF16)
        e_skip = sb("e_skip", [128, COLS])
        e_raw = sb("e_raw", [128, GB, EG])
        e_count = sb("e_count", [128, GB, EG], I32)
        e_field = sb("e_field", [128, GB, EG], I32)
        e_rank = sb("e_rank", [128, GB, EG], I32)
        e_in = sb("e_in", [128, GB, EG])
        e_off = sb("e_off", [128, GB, EG])
        e_over = sb("e_over", [128, GB, EG])
        e_far = sb("e_far", [128, GB, 1])
        e_slot = sb("e_slot", [128, GB, EG], I32)
        e_pay = sb("e_pay", [128, GB, EG], I32)
        zero_i = sb("zero_i", [128, 2 * NB], I32)
        zero_q = sb("zero_q", [128, 2 * D])
        zero_h = sb("zero_h", [128, COLS], BF16)
        upto_f = sb("upto_f", [128, 2, 128])
        count_i = sb("count_i", [1, 2, COLS], I32)
        field_i = sb("field_i", [1, 2, FIELDS, COLS], I32)
        count_f = sb("count_f", [1, FIELDS * COLS])
        most_f = sb("most_f", [1, 1])
        full_f = sb("full_f", [1, 1])
        one_col = sb("one_col", [128, 1])
        over_i = sb("over_i", [1, 1], I32)
        n_x = sb("n_x", [128, GB, EG, D])
        n_stats = sb("n_stats", [128, GB, EG, 6])
        n_mv = sb("n_mv", [128, GB, EG, 2])
        n_ln = sb("n_ln", [128, GB, EG])
        n_rstd = sb("n_rstd", [128, GB, EG])
        n_bias = sb("n_bias", [128, GB, EG])
        n_h = sb("n_h", [128, GB, EG, D])
        n_hT = sb("n_hT", [128, 2, 4 * 128])
        n_q = sb("n_q", [128, GB, EG, D])
        slot_i = sb("slot_i", [128, 2 * NB // 128, SLOTS], I32)
        slot_f = sb("slot_f", [128, NB // 128, SLOTS])
        pay_i = sb("pay_i", [SLOTS, NB], I32)
        dst_col = sb("dst_col", [SLOTS, NB], I32)
        place_i = sb("place_i", [SLOTS, NB], I32)
        place_col = sb("place_col", [SLOTS, NB])
        a_idx = sb("a_idx", [SLOTS, DEEP, 2], I32)
        a_h = sb("a_h", [SLOTS, DEEP, 2, D])
        a_q = sb("a_q", [BUCKET, DEEP, 2, D])
        a_x = sb("a_x", [BUCKET, DEEP, 2, D])
        a_hot = sb("a_hot", [SLOTS, DEEP, 2, BUCKET])
        a_off = sb("a_off", [SLOTS, 2, 2, BUCKET])
        a_T = sb("a_T", [128, 2, 4, 128])
        a_qe = sb("a_qe", [SLOTS, 2, 2, D])
        a_prod = sb("a_prod", [SLOTS, 2, 2, D])
        a_att = sb("a_att", [SLOTS, 2, 2, HEADS])
        a_clip = sb("a_clip", [SLOTS, 2, 2, HEADS])
        a_res = sb("a_res", [SLOTS, 2, 2, W])
        a_den = sb("a_den", [BUCKET, 2, 2, HEADS])
        a_inv = sb("a_inv", [BUCKET, 2, 2, HEADS])
        a_mean = sb("a_mean", [BUCKET, 2, 2, D])
        a_out = sb("a_out", [BUCKET, DEEP, 2, D])

        g_zero = sb("g_zero", [LANES, 20 * W])
        g_idx = sb("g_idx", [LANES, 2], I32)
        g_x = sb("g_x", [LANES, 2, D])
        g_acc = sb("g_acc", [LANES, W])
        g_stats = sb("g_stats", [LANES, 2, 6])
        g_mv = sb("g_mv", [LANES, 2, 2])
        g_rstd = sb("g_rstd", [LANES, 2, 2])
        g_hT = sb("g_hT", [128, 2, LANES])
        g_att = sb("g_att", [LANES, 2, HEADS])
        g_prod = sb("g_prod", [LANES, D])
        g_q = sb("g_q", [LANES, D])
        g_res = sb("g_res", [LANES, W])
        g_sb = sb("g_sb", [LANES, LANES])
        g_sel = sb("g_sel", [LANES, LANES])
        g_cnt = sb("g_cnt", [LANES, 1])
        g_to = sb("g_to", [LANES, 1], I32)
        g_new = sb("g_new", [LANES, W])
        f_acc = sb("f_acc", [LANES, RB, W])
        f_x = sb("f_x", [LANES, RB, D])
        f_r = sb("f_r", [LANES, RB, HEADS])
        f_o = sb("f_o", [LANES, RB, D])

        bank = [psum(f"bank{n}", [128, 512]) for n in range(8)]
        p_T, p_S, p_qkv, p_agg = bank[0:4]
        p_count, p_hT, p_q, p_flag = bank[0:2], bank[2:4], bank[4:6], bank[6]
        p_kv, p_aT, p_qe, p_sum = bank[0:4], bank[4:6], bank[6], bank[7]

        s_in = sem("s_in")
        s_passed = sem("s_passed")
        s_const = sem("s_const")
        s_masks = sem("s_masks")
        s_cleared = sem("s_cleared")
        s_iota = sem("s_iota")
        s_zero = sem("s_zero")
        s_qpad = sem("s_qpad")
        s_setup = sem("s_setup")
        s_ready = sem("s_ready")
        s_pad = sem("s_pad")
        s_src = sem("s_src")
        s_dst_in = sem("s_dst_in")
        s_sign = sem("s_sign")
        s_upto = sem("s_upto")
        s_bucket = sem("s_bucket")
        s_field = sem("s_field")
        s_place = sem("s_place")
        s_col = sem("s_col")
        s_payf = sem("s_payf")
        s_lin = sem("s_lin")
        s_unit = sem("s_unit")
        s_inv = sem("s_inv")
        s_first = sem("s_first")
        s_iotaf = sem("s_iotaf")
        se_hot = sem("se_hot")
        se_seen = sem("se_seen")
        se_counted = sem("se_counted")
        se_free = sem("se_free")
        se_count = sem("se_count")
        se_field = sem("se_field")
        se_rank = sem("se_rank")
        se_over = sem("se_over")
        se_in = sem("se_in")
        se_off = sem("se_off")
        se_slot = sem("se_slot")
        se_pay = sem("se_pay")
        se_flag = sem("se_flag")
        se_far = sem("se_far")
        sn_stats = sem("sn_stats")
        sn_mv = sem("sn_mv")
        sn_ln = sem("sn_ln")
        sn_rstd = sem("sn_rstd")
        sn_bias = sem("sn_bias")
        sn_h = sem("sn_h")
        sn_hT = sem("sn_hT")
        sn_hTc = sem("sn_hTc")
        sn_q = sem("sn_q")
        sn_qc = sem("sn_qc")
        s_over = sem("s_over")
        s_slotf = sem("s_slotf")
        s_slotT = sem("s_slotT")
        s_pay = sem("s_pay")
        s_placei = sem("s_placei")
        s_placed = sem("s_placed")
        s_dst = sem("s_dst")
        sa_idx = sem("sa_idx")
        sa_hot = sem("sa_hot")
        sa_T = sem("sa_T")
        sa_Tc = sem("sa_Tc")
        sa_kv = sem("sa_kv")
        sa_qe = sem("sa_qe")
        sa_qc = sem("sa_qc")
        sa_prod = sem("sa_prod")
        sa_att = sem("sa_att")
        sa_clip = sem("sa_clip")
        sa_exp = sem("sa_exp")
        sa_res = sem("sa_res")
        sa_sum = sem("sa_sum")
        sa_off = sem("sa_off")
        sa_den = sem("sa_den")
        sa_inv = sem("sa_inv")
        sa_mean = sem("sa_mean")
        sa_out = sem("sa_out")
        s_slots = [sem(f"s_slots{part}") for part in range(len(PARTS))]
        se_put = [sem(f"se_put{b}") for b in range(GB)]
        sn_x = [sem(f"sn_x{b}") for b in range(GB)]
        sn_hout = [sem(f"sn_hout{b}") for b in range(GB)]
        sn_qout = [sem(f"sn_qout{b}") for b in range(GB)]
        sa_h = [sem(f"sa_h{b}") for b in range(DEEP)]
        sa_q = [sem(f"sa_q{b}") for b in range(DEEP)]
        sa_x = [sem(f"sa_x{b}") for b in range(DEEP)]
        sa_store = [sem(f"sa_store{b}") for b in range(DEEP)]
        sg_in = sem("sg_in")
        sg_srcf = sem("sg_srcf")
        sg_zero = sem("sg_zero")
        sg_cleared = sem("sg_cleared")
        sg_idx = sem("sg_idx")
        sg_gathered = sem("sg_gathered")
        sg_scattered = sem("sg_scattered")
        sg_stats = sem("sg_stats")
        sg_mv = sem("sg_mv")
        sg_ln = sem("sg_ln")
        sg_rstd = sem("sg_rstd")
        sg_norm = sem("sg_norm")
        sg_xT = sem("sg_xT")
        sg_hT = sem("sg_hT")
        sg_qkv = sem("sg_qkv")
        sg_q = sem("sg_q")
        sg_sb = sem("sg_sb")
        sg_sT = sem("sg_sT")
        sg_sel = sem("sg_sel")
        sg_cnt = sem("sg_cnt")
        sg_to = sem("sg_to")
        sg_prod = sem("sg_prod")
        sg_att = sem("sg_att")
        sg_clip = sem("sg_clip")
        sg_exp = sem("sg_exp")
        sg_res = sem("sg_res")
        sg_agg = sem("sg_agg")
        sg_new = sem("sg_new")
        sf_done = sem("sf_done")
        sf_in = sem("sf_in")
        sf_r = sem("sf_r")
        sf_o = sem("sf_o")
        sf_out = sem("sf_out")

        block = ctx.enter_context(nc.Block())

        def hold(eng, semaphore, value):
            eng.wait_ge(semaphore, value)
            eng.sem_inc(s_passed, 1)

        def general_sync(sp):
            sp.dma_start(src_i[:], src_lanes).then_inc(sg_in, 16)
            sp.dma_start(dst_i[:], dst_lanes).then_inc(sg_in, 16)
            sp.wait_ge(sg_zero, 1)
            with sp.Fori(0, T // 20) as i:
                sp.dma_start(acc_lanes[:, bass.ds(i * (20 * W), 20 * W)], g_zero[:]).then_inc(sg_cleared, 16)
            sp.wait_ge(sf_done, 1)
            with sp.Fori(0, ROWS // RB) as i:
                sp.dma_start(f_acc[:].rearrange("p t w -> p (t w)"),
                             acc_lanes[:, bass.ds(i * (RB * W), RB * W)]).then_inc(sf_in, 16)
                sp.dma_start(f_x[:].rearrange("p t d -> p (t d)"),
                             x_lanes[:, bass.ds(i * (RB * D), RB * D)]).then_inc(sf_in, 16)
                sp.wait_ge(sf_o, 2 * i + 2)
                sp.dma_start(out_lanes[:, bass.ds(i * (RB * D), RB * D)],
                             f_o[:].rearrange("p t d -> p (t d)")).then_inc(sf_out, 16)
                hold(sp, sf_out, 16 * i + 16)

        def general_pool(pool):
            pool.wait_ge(sg_in, 32)
            pool.wait_ge(sg_cleared, 16 * (T // 20))
            with pool.Fori(0, T) as i:
                pool.tensor_copy(g_idx[:, 0:1], src_i[:, bass.ds(i, 1)]).then_inc(sg_idx, 1)
                pool.tensor_copy(g_idx[:, 1:2], dst_i[:, bass.ds(i, 1)]).then_inc(sg_idx, 1)
                hold(pool, sg_idx, 2 * i + 2)
                at_src = bass.IndirectOffsetOnAxis(ap=g_idx[:, 0:1], axis=0)
                at_dst = bass.IndirectOffsetOnAxis(ap=g_idx[:, 1:2], axis=0)
                pool.indirect_dma_start(g_x[:, 0, :], None, x, at_src).then_inc(sg_gathered, 16)
                pool.indirect_dma_start(g_x[:, 1, :], None, x, at_dst).then_inc(sg_gathered, 16)
                pool.indirect_dma_start(g_acc[:], None, acc, at_src).then_inc(sg_gathered, 16)
                pool.wait_ge(sg_to, i + 1)
                hold(pool, sg_new, i + 1)
                pool.indirect_dma_start(acc, bass.IndirectOffsetOnAxis(ap=g_to[:, 0:1], axis=0), g_new[:], None,
                                        bounds_check=N - 1, oob_is_err=False).then_inc(sg_scattered, 16)
                hold(pool, sg_scattered, 16 * i + 16)
            pool.nop().then_inc(sf_done, 1)

        def general_vector(dve):
            dve.memset(g_zero[:], 0.0).then_inc(sg_zero, 1)
            dve.wait_ge(sg_in, 32)
            dve.tensor_copy(src_f[:], src_i[:]).then_inc(sg_srcf, 1)
            dve.wait_ge(sg_srcf, 1)
            with dve.Fori(0, T) as i:
                dve.tensor_copy(g_sb[:], src_f[:, bass.ds(i, 1)].to_broadcast([LANES, LANES])).then_inc(sg_sb, 1)
                dve.wait_ge(sg_gathered, 48 * i + 48)
                for k in range(2):
                    dve.bn_stats(g_stats[:, k, :], g_x[:, k, :]).then_inc(sg_stats, 1)
                hold(dve, sg_stats, 2 * i + 2)
                for k in range(2):
                    dve.bn_aggr(g_mv[:, k, :], g_stats[:, k, :]).then_inc(sg_mv, 1)
                dve.wait_ge(sg_sT, i + 1)
                dve.tensor_scalar(g_sel[:], p_S[0:LANES, 0:LANES], g_sb[:, 0:1], None,
                                  ALU.is_equal).then_inc(sg_sel, 1)
                dve.wait_ge(sg_sel, i + 1)
                dve.tensor_tensor_reduce(g_prod[:, 0:LANES], g_sel[:], before[0:LANES, 0:LANES], 1.0, 0.0, ALU.mult,
                                         ALU.add, g_cnt[:]).then_inc(sg_cnt, 1)
                dve.wait_ge(sg_cnt, i + 1)
                dve.scalar_tensor_tensor(g_to[:], g_cnt[:], float(FAR), g_sb[:, 0:1], ALU.mult,
                                         ALU.add).then_inc(sg_to, 1)
                dve.wait_ge(sg_rstd, i + 1)
                for k in range(2):
                    dve.tensor_scalar(g_x[:, k, :], g_x[:, k, :], g_mv[:, k, 0:1], g_rstd[:, 1, k:k + 1],
                                      ALU.subtract, ALU.mult).then_inc(sg_norm, 1)
                dve.wait_ge(sg_q, i + 1)
                dve.tensor_tensor(g_prod[:], g_q[:], p_qkv[0:LANES, D:2 * D],
                                  ALU.mult).then_inc(sg_prod, 1)
                dve.wait_ge(sg_prod, i + 1)
                dve.tensor_reduce(g_att[:, 0, :], g_prod[:].rearrange("p (h d) -> p h d", h=HEADS), AX_X,
                                  ALU.add).then_inc(sg_att, 1)
                dve.wait_ge(sg_att, i + 1)
                dve.tensor_scalar(g_att[:, 1, :], g_att[:, 0, :], -CLIP, CLIP, ALU.max, ALU.min).then_inc(sg_clip, 1)
                dve.wait_ge(sg_exp, i + 1)
                dve.tensor_tensor(g_res[:, 0:D].rearrange("p (h d) -> p h d", h=HEADS),
                                  p_qkv[0:LANES, 2 * D:3 * D].rearrange("p (h d) -> p h d", h=HEADS),
                                  g_res[:, D:W].unsqueeze(2).to_broadcast([LANES, HEADS, HD]),
                                  ALU.mult).then_inc(sg_res, 1)
                dve.wait_ge(sg_agg, i + 1)
                dve.tensor_tensor(g_new[:], p_agg[0:LANES, 0:W], g_acc[:], ALU.add).then_inc(sg_new, 1)
            with dve.Fori(0, ROWS // RB) as i:
                dve.wait_ge(sf_in, 32 * i + 32)
                dve.tensor_scalar(f_r[:], f_acc[:, :, D:W], NORM_EPS, None, ALU.add).then_inc(sf_r, 1)
                dve.wait_ge(sf_r, 2 * i + 1)
                dve.reciprocal(f_r[:], f_r[:]).then_inc(sf_r, 1)
                dve.wait_ge(sf_r, 2 * i + 2)
                for t in range(RB):
                    last = dve.tensor_tensor(f_o[:, t, :].rearrange("p (h d) -> p h d", h=HEADS),
                                             f_acc[:, t, 0:D].rearrange("p (h d) -> p h d", h=HEADS),
                                             f_r[:, t, :].unsqueeze(2).to_broadcast([LANES, HEADS, HD]), ALU.mult)
                last.then_inc(sf_o, 1)
                dve.wait_ge(sf_o, 2 * i + 1)
                dve.tensor_tensor(f_o[:], f_o[:], f_x[:], ALU.add).then_inc(sf_o, 1)

        def general_scalar(act):
            with act.Fori(0, T) as i:
                act.wait_ge(sg_mv, 2 * i + 2)
                act.activation(g_rstd[:, 0, :], g_mv[:, :, 1], ACT.Ln, bias=eps_col[0:LANES, :]).then_inc(sg_ln, 1)
                act.wait_ge(sg_ln, i + 1)
                act.activation(g_rstd[:, 1, :], g_rstd[:, 0, :], ACT.Exp, scale=-0.5).then_inc(sg_rstd, 1)
                act.wait_ge(sg_xT, i + 1)
                act.activation(g_hT[:], p_T[:, 0:2 * LANES].rearrange("p (k l) -> p k l", k=2),
                               ACT.Relu).then_inc(sg_hT, 1)
                act.wait_ge(sg_qkv, i + 1)
                act.activation(g_q[:], p_qkv[0:LANES, 0:D], ACT.Copy).then_inc(sg_q, 1)
                act.wait_ge(sg_clip, i + 1)
                act.activation(g_res[:, D:W], g_att[:, 1, :], ACT.Exp).then_inc(sg_exp, 1)

        def general_tensor(pe):
            with pe.Fori(0, T) as i:
                pe.wait_ge(sg_sb, i + 1)
                pe.transpose(p_S[0:LANES, 0:LANES], g_sb[:], ident[0:LANES, 0:LANES]).then_inc(sg_sT, 1)
                pe.wait_ge(sg_norm, 2 * i + 2)
                for k in range(2):
                    last = pe.transpose(p_T[:, k * LANES:(k + 1) * LANES], g_x[:, k, :], ident[0:LANES, 0:LANES])
                last.then_inc(sg_xT, 1)
                pe.wait_ge(sg_hT, i + 1)
                pe.matmul(p_qkv[0:LANES, 0:D], g_hT[:, 0, :], q_w[:], start=True, stop=True)
                pe.matmul(p_qkv[0:LANES, D:3 * D], g_hT[:, 1, :], kv_w[:], start=True, stop=True).then_inc(sg_qkv, 1)
                pe.wait_ge(sg_res, i + 1)
                pe.wait_ge(sg_sel, i + 1)
                pe.matmul(p_agg[0:LANES, 0:W], g_sel[:], g_res[:], start=True, stop=True).then_inc(sg_agg, 1)

        def need(eng, semaphore, value):
            if not isinstance(value, int) or value > 0:
                eng.wait_ge(semaphore, value)

        def steps(eng, step, first, lo, hi, last, period):
            for k in range(first, lo):
                step(k // period, k % period)
            with eng.Fori(lo // period, hi // period) as m:
                for b in range(period):
                    step(m, b)
            for k in range(hi, last):
                step(k // period, k % period)

        def later(m, b, by, period):
            q, r = divmod(b + by, period)
            return m + q, r, period * (m + q) + r

        def there(k, count):
            return not isinstance(k, int) or 0 <= k < count

        def node_rows(dram, g, parts):
            return dram[bass.ds(g * GN, parts * EG)].rearrange("(p r) d -> p r d", r=EG)

        def parts_of(g):
            return LAST if isinstance(g, int) and g == ND else 128

        def groups(eng, step, first=0, last=NG):
            steps(eng, step, first, GB, ND - GB, last, GB)

        def later_group(g):
            return not isinstance(g, int) or g >= GB

        def load_nodes(sp, m, b, g):
            if there(g, ND + 1):
                need(sp, sn_h, EG * (g - GB + 1))
                parts = parts_of(g)
                sp.dma_start(n_x[0:parts, b], node_rows(x, g, parts)).then_inc(sn_x[b], 16)

        def sort_sync(sp):
            def step(m, b):
                load_nodes(sp, *later(m, b, 1, GB))
                m, b, g = later(m, b, -1, GB)
                if there(g, ND + 1):
                    parts = parts_of(g)
                    sp.wait_ge(sn_h, EG * g + EG)
                    sp.dma_start(node_rows(h_dram, g, parts), n_h[0:parts, b]).then_inc(sn_hout[b], 16)
                m, b, g = later(m, b, -1, GB)
                if there(g, ND + 1):
                    parts = parts_of(g)
                    sp.wait_ge(sn_qc, 2 * g + 2)
                    sp.dma_start(node_rows(q_dram, g, parts), n_q[0:parts, b]).then_inc(sn_qout[b], 16)
            groups(sp, step, last=ND + 3)

        def sort_pool(pool):
            pool.wait_ge(s_cleared, 16)
            def step(m, b):
                g = GB * m + b
                hold(pool, se_slot, g + 1)
                for j in range(EG):
                    pool.indirect_dma_start(slots, bass.IndirectOffsetOnAxis(ap=e_slot[:, b, j:j + 1], axis=0),
                                            e_pay[:, b, j:j + 1], None,
                                            bounds_check=2 * NB * SLOTS - 1, oob_is_err=False).then_inc(se_put[b], 16)
            groups(pool, step)

        def sort_vector(dve):
            EARLY = ((), (2,), (4,), (), (), (7,), (), ())
            SPREAD = ((1,), (3,), (5,), (), (6,), (), (), ())
            AT_ONCE = (range(1, 8),) + (EG - 1) * ((),)

            def hot(t, j):
                need(dve, se_free, t - NHOT + 1)
                dve.tensor_scalar(e_hot[:, j % NHOT, :], iota_b[:], col_f[:, bass.ds(t, 1)], unit_f[:, bass.ds(t, 1)],
                                  ALU.is_equal, ALU.mult).then_inc(se_hot, 1)

            def slot_of(m, b, g, part):
                at = bass.ds(EG * g, EG)
                if part == 1:
                    dve.wait_ge(se_seen, EG * g + EG)
                    dve.tensor_tensor(e_count[:, b, :], e_raw[:, b, :], inv_f[:, at], ALU.mult).then_inc(se_count, 1)
                if part == 2:
                    dve.wait_ge(se_count, g + 1)
                    dve.tensor_tensor(e_field[:, b, :], e_count[:, b, :], shift_i[:, at],
                                      ALU.logical_shift_right).then_inc(se_field, 1)
                if part == 3:
                    dve.wait_ge(se_field, g + 1)
                    dve.tensor_scalar(e_rank[:, b, :], e_field[:, b, :], 255, None,
                                      ALU.bitwise_and).then_inc(se_rank, 1)
                if part == 4:
                    dve.wait_ge(se_rank, g + 1)
                    dve.tensor_tensor(e_off[:, b, :], e_rank[:, b, :], sign[:], ALU.mult).then_inc(se_off, 1)
                    need(dve, se_flag, g - GB + 1)
                    dve.tensor_scalar(e_over[:, b, :], e_rank[:, b, :], float(SLOTS), FAR_SLOT, ALU.is_ge,
                                      ALU.mult).then_inc(se_over, 1)
                if part == 5:
                    dve.wait_ge(se_off, g + 1)
                    dve.tensor_tensor(e_in[:, b, :], e_off[:, b, :], first_f[:, at], ALU.add).then_inc(se_in, 1)
                if part == 6:
                    dve.wait_ge(se_flag, g + 1)
                    dve.tensor_reduce(e_far[:, b, :], p_flag[:, 0:EG], AX_X, ALU.max).then_inc(se_far, 1)
                if part == 7:
                    need(dve, se_put[b], 16 * EG * m)
                    dve.wait_ge(se_in, g + 1)
                    dve.wait_ge(se_far, g + 1)
                    dve.wait_ge(se_pay, g + 1)
                    dve.tensor_scalar(e_slot[:, b, :], e_in[:, b, :], e_far[:, b, :], None,
                                      ALU.add).then_inc(se_slot, 1)

            def step(m, b):
                g = GB * m + b
                m_p, b_p, g_p = later(m, b, -1, GB)
                for j in range(EG):
                    t = EG * g + j
                    if there(g_p, NG):
                        for part in EARLY[j] if later_group(g_p) else ():
                            slot_of(m_p, b_p, g_p, part)
                    if there(t + 1, ET):
                        hot(t + 1, j + 1)
                    if there(g, ND + 1):
                        parts = parts_of(g)
                        if j == 0:
                            dve.wait_ge(sn_x[b], 16 * m + 16)
                        dve.bn_stats(n_stats[0:parts, b, j, :], n_x[0:parts, b, j, :]).then_inc(sn_stats, 1)
                    if there(g_p, ND + 1):
                        parts = parts_of(g_p)
                        if j == 1:
                            hold(dve, sn_stats, EG * g_p + EG)
                            for i in range(EG):
                                dve.bn_aggr(n_mv[0:parts, b_p, i, :], n_stats[0:parts, b_p, i, :]).then_inc(sn_mv, 1)
                        if j == 4:
                            dve.wait_ge(sn_rstd, g_p + 1)
                            dve.scalar_tensor_tensor(n_bias[0:parts, b_p, :], n_mv[0:parts, b_p, :, 0], -1.0,
                                                     n_rstd[0:parts, b_p, :], ALU.mult, ALU.mult).then_inc(sn_bias, 1)
                    if there(g_p, NG):
                        for part in SPREAD[j] if later_group(g_p) else AT_ONCE[j]:
                            slot_of(m_p, b_p, g_p, part)
                    if there(t, ET):
                        need(dve, se_seen, t)
                        dve.wait_ge(se_counted, t + 1)
                        dve.tensor_tensor_reduce(e_skip[:], p_count[j % 2][:, 0:COLS], e_hot[:, j % NHOT, :], 1.0,
                                                 0.0, ALU.mult, ALU.add, e_raw[:, b, j:j + 1]).then_inc(se_seen, 1)
            hot(0, 0)
            groups(dve, step, last=ND + 3)

        def sort_scalar(act):
            def step(m, b):
                g = GB * m + b
                if there(g, NG):
                    need(act, se_put[b], 16 * EG * m)
                    act.activation(e_pay[:, b, :], pay_f[:, bass.ds(EG * g, EG)], ACT.Copy,
                                   bias=1.0).then_inc(se_pay, 1)
                m1, b1, g1 = later(m, b, -1, GB)
                m2, b2, g2 = later(m, b, -2, GB)
                if there(g1, ND + 1):
                    parts = parts_of(g1)
                    act.wait_ge(sn_mv, EG * g1 + EG)
                    act.activation(n_ln[0:parts, b1, :], n_mv[0:parts, b1, :, 1], ACT.Ln,
                                   bias=eps_col[0:parts, :]).then_inc(sn_ln, 1)
                    act.wait_ge(sn_ln, g1 + 1)
                    act.activation(n_rstd[0:parts, b1, :], n_ln[0:parts, b1, :], ACT.Exp,
                                   scale=-0.5).then_inc(sn_rstd, 1)
                if there(g2, ND + 1):
                    parts = parts_of(g2)
                    for s in range(2):
                        need(act, sn_q, 2 * g2 + s - 1)
                        act.wait_ge(sn_hT, 2 * g2 + s + 1)
                        act.activation(n_hT[:, s, 0:4 * parts], p_hT[s][:, 0:4 * parts], ACT.Copy).then_inc(sn_hTc, 1)
                if there(g1, ND + 1):
                    parts = parts_of(g1)
                    need(act, sn_hout[b1], 16 * m1)
                    act.wait_ge(sn_bias, g1 + 1)
                    for j in range(EG):
                        act.activation(n_h[0:parts, b1, j, :], n_x[0:parts, b1, j, :], ACT.Relu,
                                       bias=n_bias[0:parts, b1, j:j + 1],
                                       scale=n_rstd[0:parts, b1, j:j + 1]).then_inc(sn_h, 1)
                if there(g2, ND + 1):
                    parts = parts_of(g2)
                    need(act, sn_qout[b2], 16 * m2)
                    for s in range(2):
                        act.wait_ge(sn_q, 2 * g2 + s + 1)
                        act.activation(n_q[0:parts, b2, 4 * s:4 * s + 4, :],
                                       p_q[s][0:parts, :].rearrange("p (r d) -> p r d", d=D),
                                       ACT.Copy).then_inc(sn_qc, 1)
            groups(act, step, last=ND + 3)

        def sort_tensor(pe):
            def count(t, j, part, wait_for, to_signal):
                pe.wait_ge(*wait_for)
                pe.matmul(p_count[j % 2][:, 0:COLS], upto[:, part, :], e_hot[:, j % NHOT, :], start=False,
                          stop=True, skip_group_check=True).then_inc(to_signal, 1)

            def step(m, b):
                g = GB * m + b
                m2, b2, g2 = later(m, b, -2, GB)
                dense = there(g2, ND + 1)
                parts = parts_of(g2)
                m1, b1, g1 = later(m, b, -1, GB)
                for j in range(EG):
                    t = EG * g + j
                    if there(g1, NG) and j == (3 if later_group(g1) else 0):
                        pe.wait_ge(se_over, g1 + 1)
                        need(pe, se_far, g1)
                        pe.matmul(p_flag[:, 0:EG], all_ones[:], e_over[:, b1, :], start=False, stop=True,
                                  skip_group_check=True).then_inc(se_flag, 1)
                    if there(t + 1, ET):
                        count(t + 1, j + 1, 0, (se_hot, t + 2), se_counted)
                    if dense and j in (1, 2):
                        s = j - 1
                        need(pe, sn_hTc, 2 * g2 + s - 1)
                        pe.wait_ge(sn_h, EG * g2 + 4 * s + 4)
                        for i in range(4):
                            last = pe.transpose(p_hT[s][:, i * parts:(i + 1) * parts], n_h[0:parts, b2, 4 * s + i, :],
                                                ident[0:parts, 0:parts])
                        last.then_inc(sn_hT, 1)
                    if dense and j >= 4:
                        s = (j - 4) // 2
                        if j % 2 == 0:
                            need(pe, sn_qc, 2 * g2 + s - 1)
                            pe.wait_ge(sn_hTc, 2 * g2 + s + 1)
                        for i in range(j % 2 * 2, j % 2 * 2 + 2):
                            last = pe.matmul(p_q[s][0:parts, i * D:(i + 1) * D], n_hT[:, s, i * parts:(i + 1) * parts],
                                             q_w[:], start=True, stop=True)
                        if j % 2:
                            last.then_inc(sn_q, 1)
                    if there(t, ET):
                        count(t, j, 1, (se_seen, t + 1), se_free)

            for c in range(2):
                pe.matmul(p_count[c][:, 0:COLS], upto[:, 0, :], zero_h[:], start=True, stop=True)
            pe.matmul(p_flag[:, 0:EG], all_ones[:], zero_q[:, 0:EG], start=True, stop=True)
            count(0, 0, 0, (se_hot, 1), se_counted)
            groups(pe, step, last=ND + 3)

        def attend(eng, step, first=0, last=NP):
            steps(eng, step, first, DEEP, NP - DEEP, last, DEEP)

        def two_buckets(dram, k):
            return dram[bass.ds(k * 2 * BUCKET, 2 * BUCKET)].rearrange("(j n) d -> n j d", j=2)

        def attend_sync(sp):
            for part, (lo, hi) in enumerate(PARTS):
                for table in (0, NC):
                    sp.dma_start(slot_i[:, table + lo:table + hi], slot_rows[:, table + lo:table + hi]
                                 ).then_inc(s_slots[part], 16)

            def step(m, b):
                mq, bq, kq = later(m, b, 5, DEEP)
                if there(kq, NP):
                    need(sp, sa_qe, kq - DEEP + 1)
                    sp.dma_start(a_q[:, bq], two_buckets(q_dram, kq)).then_inc(sa_q[bq], 16)
                mx, bx, kx = later(m, b, 2, DEEP)
                if there(kx, NP):
                    need(sp, sa_out, kx - DEEP + 1)
                    if isinstance(kx, int) and kx == NP - 1:
                        sp.dma_start(a_x[0:TAIL, bx, 0, :], x[N - TAIL:N]).then_inc(sa_x[bx], 16)
                    else:
                        sp.dma_start(a_x[:, bx], two_buckets(x, kx)).then_inc(sa_x[bx], 16)
                mo, bo, ko = later(m, b, -2, DEEP)
                if there(ko, NP):
                    sp.wait_ge(sa_out, ko + 1)
                    if isinstance(ko, int) and ko == NP - 1:
                        sp.dma_start(out[N - TAIL:N], a_out[0:TAIL, bo, 0, :]).then_inc(sa_store[bo], 16)
                    else:
                        sp.dma_start(two_buckets(out, ko), a_out[:, bo]).then_inc(sa_store[bo], 16)
            attend(sp, step, first=-5, last=NP + 2)
            for b in range(DEEP):
                sp.wait_ge(sa_store[b], 16 * (NP // DEEP))

        def attend_pool(pool):
            for b in range(GB):
                pool.wait_ge(sn_hout[b], 16 * len(range(b, ND + 1, GB)))

            def step(m, b):
                k = DEEP * m + b
                hold(pool, sa_idx, k + 1)
                for j in range(2):
                    pool.indirect_dma_start(a_h[:, b, j, :], None, h_dram,
                                            bass.IndirectOffsetOnAxis(ap=a_idx[:, b, j:j + 1], axis=0)
                                            ).then_inc(sa_h[b], 16)
            attend(pool, step)

        def attend_vector(dve):
            for part, (lo, hi) in enumerate(PARTS):
                at = slice(128 * lo, 128 * hi)
                dve.wait_ge(s_slots[part], 32)
                dve.tensor_tensor(slot_f[:, lo:hi], slot_i[:, lo:hi], slot_i[:, NC + lo:NC + hi],
                                  ALU.add).then_inc(s_slotf, 1)
                dve.wait_ge(s_slotT, part + 1)
                dve.tensor_copy(pay_i[:, at], bank[6 + part][:, 0:128 * (hi - lo)]).then_inc(s_pay, 1)
                dve.wait_ge(s_pay, part + 1)
                dve.tensor_scalar(dst_col[:, at], pay_i[:, at], 7, None, ALU.logical_shift_right).then_inc(s_dst, 1)
                dve.tensor_scalar(place_i[:, at], pay_i[:, at], 127, None, ALU.bitwise_and).then_inc(s_placei, 1)
            dve.wait_ge(s_placei, len(PARTS))
            dve.tensor_copy(place_col[:], place_i[:]).then_inc(s_placed, 1)

            def step(m, b):
                k, c = DEEP * m + b, b % 2
                mp, bp, kp = later(m, b, -1, DEEP)
                cp = bp % 2
                now, before_ = there(k, NP), there(kp, NP)
                heads = "p j (h d) -> p (j h) d"
                if now:
                    dve.wait_ge(sa_kv, k + 1)
                    dve.wait_ge(sa_qc, k + 1)
                    dve.tensor_tensor(a_prod[:, c], p_kv[b % 4][:].rearrange("p (j w) -> p j w", j=2)[:, :, 0:D],
                                      a_qe[:, c], ALU.mult).then_inc(sa_prod, 1)
                p_prev = p_sum[0:BUCKET, 0:2 * W].rearrange("p (j w) -> p j w", j=2)
                mo, bo, ko = later(m, b, -2, DEEP)
                if there(ko, NP):
                    dve.wait_ge(sa_x[bo], 16 * mo + 16)
                    need(dve, sa_store[bo], 16 * mo)
                    dve.wait_ge(sa_mean, ko + 1)
                    dve.tensor_tensor(a_out[:, bo], a_mean[:, c], a_x[:, bo], ALU.add).then_inc(sa_out, 1)
                if now:
                    dve.wait_ge(sa_prod, k + 1)
                    dve.tensor_reduce(a_att[:, c].rearrange("p j h -> p (j h)"),
                                      a_prod[:, c].rearrange("p j (h d) -> p (j h) d", h=HEADS),
                                      AX_X, ALU.add).then_inc(sa_att, 1)
                if before_:
                    dve.wait_ge(sa_sum, kp + 1)
                    dve.tensor_scalar(a_den[:, cp], p_prev[:, :, D:W], NORM_EPS, None, ALU.add).then_inc(sa_den, 1)
                if now:
                    dve.wait_ge(sa_att, k + 1)
                    dve.tensor_scalar(a_clip[:, c], a_att[:, c], -CLIP, CLIP, ALU.max, ALU.min).then_inc(sa_clip, 1)
                if before_:
                    dve.wait_ge(sa_den, kp + 1)
                    dve.reciprocal(a_inv[:, cp], a_den[:, cp]).then_inc(sa_inv, 1)
                    dve.wait_ge(sa_inv, kp + 1)
                    dve.tensor_tensor(a_mean[:, cp].rearrange("p j (h d) -> p j h d", h=HEADS),
                                      p_prev[:, :, 0:D].rearrange("p j (h d) -> p j h d", h=HEADS),
                                      a_inv[:, cp].unsqueeze(3).to_broadcast([BUCKET, 2, HEADS, HD]),
                                      ALU.mult).then_inc(sa_mean, 1)
                if now:
                    dve.wait_ge(sa_exp, k + 1)
                    dve.tensor_tensor(a_res[:, c, :, 0:D].rearrange("p j (h d) -> p j h d", h=HEADS),
                                      p_kv[b % 4][:].rearrange("p (j w) -> p j w", j=2)[:, :, D:2 * D]
                                      .rearrange("p j (h d) -> p j h d", h=HEADS),
                                      a_res[:, c, :, D:W].unsqueeze(3).to_broadcast([SLOTS, 2, HEADS, HD]),
                                      ALU.mult).then_inc(sa_res, 1)
            attend(dve, step, last=NP + 2)

        def attend_scalar(act):
            def step(m, b):
                k = DEEP * m + b
                if there(k, NP):
                    need(act, sa_sum, k - 1)
                    act.wait_ge(sa_clip, k + 1)
                    act.activation(a_res[:, b % 2, :, D:W], a_clip[:, b % 2], ACT.Exp).then_inc(sa_exp, 1)
                mq, bq, kq = later(m, b, 2, DEEP)
                if there(kq, NP):
                    need(act, sa_prod, kq - 1)
                    act.wait_ge(sa_qe, kq + 1)
                    act.activation(a_qe[:, bq % 2], p_qe[:, 0:2 * D].rearrange("p (j d) -> p j d", j=2),
                                   ACT.Copy).then_inc(sa_qc, 1)
                mh, bh, kh = later(m, b, 3, DEEP)
                if there(kh, NP):
                    need(act, sa_kv, kh - 1)
                    act.wait_ge(sa_T, kh + 1)
                    act.activation(a_T[:, bh % 2].rearrange("p a b -> p (a b)"), p_aT[bh % 2][:],
                                   ACT.Copy).then_inc(sa_Tc, 1)
                mh, bh, kh = later(m, b, 4, DEEP)
                if there(kh, NP):
                    if isinstance(kh, int) and kh == 0:
                        act.wait_ge(s_placed, 1)
                    need(act, sa_hot, kh - 1)
                    for j in range(2):
                        act.activation(a_off[:, bh % 2, j, :], iota_f[:], ACT.Abs, scale=-1.0,
                                       bias=place_col[:, bass.ds(2 * kh + j, 1)]).then_inc(sa_off, 1)
                    need(act, sa_sum, kh - DEEP + 1)
                    act.wait_ge(sa_off, 2 * kh + 2)
                    act.activation(a_hot[:, bh].rearrange("p a b -> p (a b)"),
                                   a_off[:, bh % 2].rearrange("p a b -> p (a b)"), ACT.Relu, scale=-1.0,
                                   bias=one_col[:]).then_inc(sa_hot, 1)
                mi, bi, ki = later(m, b, 6, DEEP)
                if there(ki, NP):
                    if isinstance(ki, int) and ki in (0, 2):
                        act.wait_ge(s_dst, 1 + ki // 2)
                    need(act, sa_T, ki - DEEP + 1)
                    act.activation(a_idx[:, bi, :], dst_col[:, bass.ds(2 * ki, 2)], ACT.Copy).then_inc(sa_idx, 1)
            attend(act, step, first=-6)

        def attend_tensor(pe):
            for part, (lo, hi) in enumerate(PARTS):
                pe.wait_ge(s_slotf, part + 1)
                for c in range(lo, hi):
                    last = pe.transpose(bank[6 + part][:, (c - lo) * 128:(c - lo + 1) * 128], slot_f[:, c, :], ident[:])
                last.then_inc(s_slotT, 1)

            def step(m, b):
                mp, bp, kp = later(m, b, -1, DEEP)
                if there(kp, NP):
                    c = bp % 2
                    need(pe, sa_mean, kp)
                    pe.wait_ge(sa_res, kp + 1)
                    for j in range(2):
                        last = pe.matmul(p_sum[0:BUCKET, j * W:(j + 1) * W], a_hot[:, bp, j, :],
                                         a_res[:, c, j, :], start=True, stop=True)
                    last.then_inc(sa_sum, 1)
                mq, bq, kq = later(m, b, 2, DEEP)
                if there(kq, NP):
                    c = bq % 2
                    need(pe, sa_qc, kq)
                    pe.wait_ge(sa_Tc, kq + 1)
                    pe.wait_ge(sa_q[bq], 16 * mq + 16)
                    for j in range(2):
                        last = pe.matmul(p_qe[:, j * D:(j + 1) * D], a_T[0:BUCKET, c, 2 + j, :], a_q[:, bq, j, :],
                                         start=True, stop=True)
                    last.then_inc(sa_qe, 1)
                mh, bh, kh = later(m, b, 3, DEEP)
                if there(kh, NP):
                    need(pe, sa_Tc, kh - 1)
                    pe.wait_ge(sa_h[bh], 32 * mh + 32)
                    for j in range(2):
                        pe.transpose(p_aT[bh % 2][:, j * 128:(j + 1) * 128], a_h[:, bh, j, :], ident[:])
                    pe.wait_ge(sa_hot, kh + 1)
                    for j in range(2):
                        last = pe.transpose(p_aT[bh % 2][0:BUCKET, (2 + j) * 128:(3 + j) * 128], a_hot[:, bh, j, :],
                                            ident[:])
                    last.then_inc(sa_T, 1)
                if there(kq, NP):
                    need(pe, sa_res, kq - 3)
                    for j in range(2):
                        last = pe.matmul(p_kv[bq % 4][:, j * 2 * D:(j + 1) * 2 * D], a_T[:, bq % 2, j, :], kv_w[:],
                                         start=True, stop=True)
                    last.then_inc(sa_kv, 1)
            attend(pe, step, first=-3, last=NP + 1)

        def either(eng, general, fast):
            eng.wait_ge(s_over, 1)
            over = eng.value_load(over_i[0:1, 0:1], min_val=0, max_val=1)
            with eng.If(over > 0):
                general(eng)
            with eng.Else():
                fast(eng)

        @block.sync
        def _(sp):
            sp.wait_ge(s_pad, 2)
            for e, edges, signal in ((e_src, src, s_src), (e_dst, dst, s_dst_in)):
                sp.dma_start(e[:, 0:FULL], edges[0:128 * FULL].rearrange("(p t) -> p t", p=128)).then_inc(signal, 16)
                sp.dma_start(e[0:REST, FULL:FULL + 1], edges[128 * FULL:E].rearrange("(p t) -> p t", t=1)
                             ).then_inc(signal, 16)
            load_nodes(sp, 0, 0, 0)
            sp.wait_ge(s_zero, 6)
            sp.dma_start(slot_rows, zero_i[:].rearrange("b (c s) -> b c s", s=SLOTS)).then_inc(s_cleared, 16)
            sp.dma_start(q_dram[N:NB * BUCKET], zero_q[0:(NB * BUCKET - N) // 2].rearrange("p (r d) -> p r d", r=2)
                         ).then_inc(s_qpad, 16)
            sp.dma_start(q_w[:], qW).then_inc(s_in, 16)
            sp.dma_start(kv_w[:, 0:D], kW).then_inc(s_in, 16)
            sp.dma_start(kv_w[:, D:2 * D], vW).then_inc(s_in, 16)
            sort_sync(sp)
            sp.wait_ge(s_qpad, 16)
            for b in range(GB):
                sp.wait_ge(se_put[b], 16 * EG * len(range(b, NG, GB)))
                sp.wait_ge(sn_hout[b], 16 * len(range(b, ND + 1, GB)))
                sp.wait_ge(sn_qout[b], 16 * len(range(b, ND + 1, GB)))
            either(sp, general_sync, attend_sync)

        @block.gpsimd
        def _(pool):
            pool.memset(ident[:], 1.0).then_inc(s_const, 1)
            pool.memset(before[:], 1.0).then_inc(s_const, 1)
            pool.memset(upto_f[:], 1.0).then_inc(s_const, 1)
            pool.memset(all_ones[:], 1.0).then_inc(s_const, 1)
            pool.wait_ge(s_const, 4)
            pool.affine_select(out=ident[:], in_=ident[:], compare_op=ALU.is_equal, fill=0.0, base=0,
                               pattern=[[-1, 128]], channel_multiplier=1).then_inc(s_masks, 1)
            pool.affine_select(out=before[:], in_=before[:], compare_op=ALU.is_gt, fill=0.0, base=0,
                               pattern=[[-1, 128]], channel_multiplier=1).then_inc(s_masks, 1)
            pool.affine_select(out=upto_f[:, 0, :], in_=upto_f[:, 0, :], compare_op=ALU.is_gt, fill=0.0, base=0,
                               pattern=[[1, 128]], channel_multiplier=-1).then_inc(s_masks, 1)
            pool.affine_select(out=upto_f[:, 1, :], in_=upto_f[:, 1, :], compare_op=ALU.is_ge, fill=0.0, base=0,
                               pattern=[[-1, 128]], channel_multiplier=1).then_inc(s_masks, 1)
            pool.iota(iota_i[:], pattern=[[1, COLS]], base=0, channel_multiplier=0).then_inc(s_iota, 1)
            pool.wait_ge(s_masks, 4)
            sort_pool(pool)
            either(pool, general_pool, attend_pool)

        @block.vector
        def _(dve):
            def then(ins):
                chained[0] += 1
                ins.then_inc(s_setup, 1)
                dve.wait_ge(s_setup, chained[0])
            chained = [0]
            dve.memset(e_src[:, FULL:ET], NO_NODE).then_inc(s_pad, 1)
            dve.memset(e_dst[:, FULL:ET], 0).then_inc(s_pad, 1)
            dve.memset(zero_i[:], 0).then_inc(s_zero, 1)
            dve.memset(zero_q[:], 0.0).then_inc(s_zero, 1)
            dve.memset(zero_h[:], 0.0).then_inc(s_zero, 1)
            dve.memset(eps_col[:], LN_EPS).then_inc(s_zero, 1)
            dve.memset(one_col[:], 1.0).then_inc(s_zero, 1)
            dve.memset(sign[:], 1.0).then_inc(s_zero, 1)
            dve.wait_ge(s_zero, 6)
            dve.memset(sign[:].rearrange("p (t c) -> p t c", c=2)[:, :, 1:2], -1.0).then_inc(s_sign, 1)
            dve.wait_ge(s_masks, 4)
            dve.tensor_copy(upto[:], upto_f[:]).then_inc(s_upto, 1)
            dve.wait_ge(s_iota, 1)
            dve.tensor_copy(iota_b[:], iota_i[:]).then_inc(s_upto, 1)
            dve.wait_ge(s_src, 32)
            then(dve.tensor_scalar(mid_f[:], e_src[:], 1.0 / BUCKET, 0.5 / BUCKET - 0.5, ALU.mult, ALU.add))
            then(dve.tensor_scalar(mid_f[:], mid_f[:], ROUND, None, ALU.add))
            dve.tensor_scalar(bucket_f[:], mid_f[:], -ROUND, None, ALU.add).then_inc(s_bucket, 1)
            dve.wait_ge(s_bucket, 1)
            then(dve.tensor_scalar(last_f[:], bucket_f[:], 2.0 * COLS, None, ALU.is_ge))
            dve.scalar_tensor_tensor(field_f[:], bucket_f[:], float(COLS), last_f[:], ALU.is_ge,
                                     ALU.add).then_inc(s_field, 1)
            dve.scalar_tensor_tensor(place_f[:], bucket_f[:], -float(BUCKET), e_src[:], ALU.mult,
                                     ALU.add).then_inc(s_place, 1)
            dve.wait_ge(s_field, 1)
            dve.scalar_tensor_tensor(col_f[:], field_f[:], -float(COLS), bucket_f[:], ALU.mult,
                                     ALU.add).then_inc(s_col, 1)
            dve.wait_ge(s_dst_in, 32)
            dve.wait_ge(s_place, 1)
            dve.scalar_tensor_tensor(pay_f[:], e_dst[:], 128.0, place_f[:], ALU.mult, ALU.add).then_inc(s_payf, 1)
            dve.wait_ge(s_lin, 1)
            dve.scalar_tensor_tensor(unit_f[:], last_f[:], 65025.0, unit_lin[:], ALU.mult, ALU.add).then_inc(s_unit, 1)
            dve.wait_ge(s_lin, 2)
            dve.scalar_tensor_tensor(inv_f[:], last_f[:], 65025.0 / 65536, inv_lin[:], ALU.mult,
                                     ALU.add).then_inc(s_inv, 1)
            dve.wait_ge(s_sign, 1)
            dve.wait_ge(s_upto, 2)
            dve.wait_ge(s_col, 1)
            dve.wait_ge(s_payf, 1)
            dve.wait_ge(s_unit, 1)
            dve.wait_ge(s_inv, 1)
            dve.wait_ge(s_first, 3)
            dve.nop().then_inc(s_ready, 1)
            sort_vector(dve)
            dve.wait_ge(se_free, ET)
            for c in range(2):
                then(dve.tensor_copy(count_i[:, c, :], p_count[c][0:1, 0:COLS]))
            for f in range(FIELDS):
                then(dve.tensor_scalar(field_i[:, :, f, :], count_i[:], 8 * f, 255, ALU.logical_shift_right,
                                       ALU.bitwise_and))
            then(dve.tensor_tensor(count_f[:], field_i[:, 0].rearrange("p f c -> p (f c)"),
                                   field_i[:, 1].rearrange("p f c -> p (f c)"), ALU.add))
            then(dve.tensor_reduce(most_f[:], count_f[:], AX_X, ALU.max))
            then(dve.tensor_scalar(full_f[:], most_f[:], float(SLOTS), None, ALU.is_gt))
            dve.scalar_tensor_tensor(over_i[:], e_far[0:1, (NG - 1) % GB, :], 0.0, full_f[:], ALU.is_gt,
                                     ALU.max).then_inc(s_over, 1)
            either(dve, general_vector, attend_vector)

        @block.scalar
        def _(act):
            act.preload_act_table_set("natural_log_exp_and_others")
            act.wait_ge(s_iota, 1)
            act.activation(iota_f[:], iota_i[:, 0:BUCKET], ACT.Copy, bias=1.0).then_inc(s_iotaf, 1)
            act.wait_ge(s_bucket, 1)
            act.activation(first_f[:], bucket_f[:], ACT.Copy, scale=float(SLOTS)).then_inc(s_first, 1)
            act.wait_ge(s_field, 1)
            act.activation(unit_lin[:], field_f[:], ACT.Copy, scale=255.0, bias=1.0).then_inc(s_lin, 1)
            act.activation(inv_lin[:], field_f[:], ACT.Copy, scale=-255.0 / 256, bias=1.0).then_inc(s_lin, 1)
            act.activation(shift_i[:], field_f[:], ACT.Copy, scale=8.0).then_inc(s_first, 1)
            odd = first_f[:].rearrange("p (t c) -> p t c", c=2)[:, :, 1]
            act.wait_ge(s_first, 1)
            act.activation(odd, odd, ACT.Copy, bias=NB * SLOTS + SLOTS - 1.0).then_inc(s_first, 1)
            act.wait_ge(s_ready, 1)
            sort_scalar(act)
            either(act, general_scalar, attend_scalar)

        @block.tensor
        def _(pe):
            pe.wait_ge(s_ready, 1)
            pe.wait_ge(s_in, 48)
            sort_tensor(pe)
            pe.wait_ge(sn_hTc, 2 * (ND + 1))
            pe.wait_ge(sn_qc, 2 * (ND + 1))
            either(pe, general_tensor, attend_tensor)


def kernel(x, src, dst, L0_gnn_qW, L0_gnn_kW, L0_gnn_vW):
    import numpy as np
    import concourse.bacc as bacc
    from concourse.bass_utils import run_bass_kernel_spmd

    nc = bacc.Bacc("TRN2", target_bir_lowering=False, num_devices=1)
    given = {"x": x, "src": src, "dst": dst, "qW": L0_gnn_qW, "kW": L0_gnn_kW, "vW": L0_gnn_vW}
    arrays, aps = {}, {}
    for name, a in given.items():
        a = np.ascontiguousarray(a)
        arrays[f"in_{name}"] = a
        aps[name] = nc.dram_tensor(f"in_{name}", a.shape, mybir.dt.from_np(a.dtype), kind="ExternalInput").ap()
    out = nc.dram_tensor("out", list(x.shape), F32, kind="ExternalOutput").ap()
    gnn_kernel(nc, aps["x"], aps["src"], aps["dst"], aps["qW"], aps["kW"], aps["vW"], out)
    r = run_bass_kernel_spmd(nc, [arrays], core_ids=[0])
    return r.results[0]["out"]
```
